# Optimizing a Trainium2 kernel written in Bass

```python
import numpy as np
import jax
import jax.numpy as jnp

def _softmax(x, axis=-1):
    return jax.nn.softmax(x, axis=axis)

def _gelu(x):
    return jax.nn.gelu(x, approximate=True)

def _silu(x):
    return jax.nn.silu(x)

def _sigmoid(x):
    return jax.nn.sigmoid(x)

def _layernorm(x, axis=-1, eps=1e-05):
    m = jnp.mean(x, axis=axis, keepdims=True)
    v = jnp.var(x, axis=axis, keepdims=True)
    return (x - m) / jnp.sqrt(v + eps)

def _scatter_add(tgt, idx, src, axis=0):
    return tgt.at[idx].add(src)

def _segment_sum(src, seg, n):
    return jax.ops.segment_sum(src, seg, n)
kernel_name = 'mk_xattn_ffn_d4_seqx_r8_81a8c9'

def setup_inputs(seed: int=0):
    np.random.seed(seed)
    _w = jnp.asarray

    def _rec_inputs():
        import jax
        import jax.numpy as jnp
        _rk = jax.random.key(seed)
        x = -0.0003929 + 0.9999 * jax.random.normal(jax.random.fold_in(_rk, 1), (8, 128, 512), jnp.float32)
        _lenS = 128 - jax.random.randint(jax.random.fold_in(_rk, 7), (8,), 0, max(1, 128 // 4) + 1, jnp.int32)
        _lenS2 = 128 - jax.random.randint(jax.random.fold_in(_rk, 8), (8,), 0, max(1, 128 // 4) + 1, jnp.int32)
        _ctx_4096P = jax.random.normal(jax.random.fold_in(_rk, 11), (8, 16, 512), jnp.float32)
        _ctx_4096c = jax.random.dirichlet(jax.random.fold_in(_rk, 511), 0.3 * jnp.ones((16,), jnp.float32), (8, 128))
        _ctx_4096t = jnp.einsum('bsk,bkd->bsd', _ctx_4096c, _ctx_4096P)
        _ctx_4096t = _ctx_4096t * jax.lax.rsqrt(jnp.mean(jnp.square(_ctx_4096t)) + 1e-12) * 0.953939
        ctx_4096 = 2.81802e-05 + 1.00001 * (_ctx_4096t + 0.3 * jax.random.normal(jax.random.fold_in(_rk, 611), (8, 128, 512), jnp.float32))
        itok_BxS2_0_2047 = jax.random.randint(jax.random.fold_in(_rk, 12), (8, 128), 0, 256, jnp.int32)
        _validS = jnp.arange(128)[None, :] < _lenS[:, None]
        _validS2 = jnp.arange(128)[None, :] < _lenS2[:, None]
        _causal = jnp.tril(jnp.ones((128, 128), dtype=bool))
        mask_1x1xSxS2_ff0 = jnp.where(jnp.ones((1, 1, 128, 128), dtype=bool), 0.0, -1000000000.0).astype(jnp.float32)
        return (x, ctx_4096, itok_BxS2_0_2047, mask_1x1xSxS2_ff0)
    x, ctx_4096, itok_BxS2_0_2047, mask_1x1xSxS2_ff0 = _rec_inputs()

    def _L0_xattn_setup():
        import jax, jax.numpy as jnp
        import numpy as np
        HIDDEN = 512
        N_HEADS = 32
        N_KV_HEADS = 8
        HEAD_DIM = HIDDEN // N_HEADS
        N_REP = N_HEADS // N_KV_HEADS
        ROPE_THETA = 10000.0
        B, S = (2, 256)

        def _rotate_half(x):
            x1, x2 = jnp.split(x, 2, axis=-1)
            return jnp.concatenate((-x2, x1), axis=-1)

        def _rope_cos_sin(position_ids):
            inv_freq = 1.0 / ROPE_THETA ** (jnp.arange(0, HEAD_DIM, 2, dtype=jnp.float32) / HEAD_DIM)
            freqs = position_ids[..., None].astype(jnp.float32) * inv_freq
            emb = jnp.concatenate((freqs, freqs), axis=-1)
            return (jnp.cos(emb)[:, None, :, :], jnp.sin(emb)[:, None, :, :])
        key = jax.random.key(seed)
        ks = jax.random.split(key, 9)
        sc = 1.0 / np.sqrt(HIDDEN)
        query = jax.random.normal(ks[0], (B, S, HIDDEN), jnp.float32)
        key_t = jax.random.normal(ks[1], (B, S, HIDDEN), jnp.float32)
        value = jax.random.normal(ks[2], (B, S, HIDDEN), jnp.float32)
        position_ids = jnp.sort(jax.random.randint(ks[3], (B, S), 0, S), axis=-1)
        Wq = jax.random.normal(ks[4], (HIDDEN, N_HEADS * HEAD_DIM), jnp.float32) * sc
        Wk = jax.random.normal(ks[5], (HIDDEN, N_KV_HEADS * HEAD_DIM), jnp.float32) * sc
        Wv = jax.random.normal(ks[6], (HIDDEN, N_KV_HEADS * HEAD_DIM), jnp.float32) * sc
        Wo = jax.random.normal(ks[7], (N_HEADS * HEAD_DIM, HIDDEN), jnp.float32) * sc
        return {'query': query, 'key': key_t, 'value': value, 'position_ids': position_ids, 'Wq': Wq, 'Wk': Wk, 'Wv': Wv, 'Wo': Wo}
    _L0_xattn_all = _L0_xattn_setup()
    _L0_xattn_in = {k: v for k, v in _L0_xattn_all.items() if k in ('Wq', 'Wk', 'Wv', 'Wo')}
    del _L0_xattn_all

    def _L0_ffn_setup():
        import jax, jax.numpy as jnp
        import numpy as np
        H, FF = (512, 1792)
        B, S = (4, 256)
        key = jax.random.key(seed)
        ks = jax.random.split(key, 7)
        x = jax.random.normal(ks[0], (B, S, H), dtype=jnp.float32)
        gate_t = jax.random.randint(ks[1], (FF, H), -1, 2, dtype=jnp.int32)
        up_t = jax.random.randint(ks[2], (FF, H), -1, 2, dtype=jnp.int32)
        down_t = jax.random.randint(ks[3], (H, FF), -1, 2, dtype=jnp.int32)
        gate_s = jax.random.uniform(ks[4], (FF,), jnp.float32, 0.01, 0.1)
        up_s = jax.random.uniform(ks[5], (FF,), jnp.float32, 0.01, 0.1)
        down_s = jax.random.uniform(ks[6], (H,), jnp.float32, 0.01, 0.1)
        return {'x': x, 'gate_t': gate_t, 'up_t': up_t, 'down_t': down_t, 'gate_s': gate_s, 'up_s': up_s, 'down_s': down_s}
    _L0_ffn_all = _L0_ffn_setup()
    _L0_ffn_in = {k: v for k, v in _L0_ffn_all.items() if k in ('gate_t', 'up_t', 'down_t', 'gate_s', 'up_s', 'down_s')}
    del _L0_ffn_all

    def _L1_xattn_setup():
        import jax, jax.numpy as jnp
        import numpy as np
        HEADS = 32
        KV_HEADS = 8
        HEAD_DIM = 128
        EPS = 1e-06

        def rms_norm(x, w):
            var = jnp.mean(jnp.square(x.astype(jnp.float32)), axis=-1, keepdims=True)
            return (x.astype(jnp.float32) * jax.lax.rsqrt(var + EPS)).astype(x.dtype) * w
        key = jax.random.key(seed)
        ks = jax.random.split(key, 6)
        bsz, n_lat, seq, hidden = (8, 64, 512, 512)
        return {'latents': jax.random.normal(ks[0], (bsz, n_lat, hidden), jnp.float32), 'context': jax.random.normal(ks[1], (bsz, seq, hidden), jnp.float32), 'Wq': jax.random.normal(ks[2], (hidden, HEADS * HEAD_DIM), jnp.float32) * 0.02, 'Wk': jax.random.normal(ks[3], (hidden, KV_HEADS * HEAD_DIM), jnp.float32) * 0.02, 'Wv': jax.random.normal(ks[4], (hidden, KV_HEADS * HEAD_DIM), jnp.float32) * 0.02, 'Wo': jax.random.normal(ks[5], (HEADS * HEAD_DIM, hidden), jnp.float32) * 0.02, 'q_norm_w': jnp.ones((HEAD_DIM,), jnp.float32), 'k_norm_w': jnp.ones((HEAD_DIM,), jnp.float32)}
    _L1_xattn_all = _L1_xattn_setup()
    _L1_xattn_in = {k: v for k, v in _L1_xattn_all.items() if k in ('Wq', 'Wk', 'Wv', 'Wo', 'q_norm_w', 'k_norm_w')}
    del _L1_xattn_all

    def _L1_ffn_setup():
        import jax, jax.numpy as jnp
        import numpy as np
        B_, S, D = (4, 512, 512)
        E, R, O = (8, 16, 512)
        TOP_K = 2
        SCALING = 8.0 / R
        key = jax.random.key(seed)
        ks = jax.random.split(key, 5)
        x = jax.random.normal(ks[0], (B_, S, D), dtype=jnp.float32)
        router_w = jax.random.normal(ks[1], (E, D), dtype=jnp.float32) * (1.0 / np.sqrt(D))
        router_b = jax.random.normal(ks[2], (E,), dtype=jnp.float32) * 0.01
        A = jax.random.normal(ks[3], (E, R, D), dtype=jnp.float32) * (1.0 / np.sqrt(D))
        Bm = jax.random.normal(ks[4], (E, O, R), dtype=jnp.float32) * 0.02
        return {'x': x, 'router_w': router_w, 'router_b': router_b, 'A': A, 'Bm': Bm}
    _L1_ffn_all = _L1_ffn_setup()
    _L1_ffn_in = {k: v for k, v in _L1_ffn_all.items() if k in ('router_w', 'router_b', 'A', 'Bm')}
    del _L1_ffn_all

    def _L2_xattn_setup():
        import jax, jax.numpy as jnp
        import numpy as np
        DIM = 512
        NUM_HEADS = 32
        NUM_KV_HEADS = 8
        HEAD_DIM = DIM // NUM_HEADS
        KV_DIM = DIM // (NUM_HEADS // NUM_KV_HEADS)
        B, S = (1, 256)
        key = jax.random.key(seed)
        ks = jax.random.split(key, 7)
        w_scale = DIM ** (-0.5)
        return {'query': jax.random.normal(ks[0], (B, S, DIM), jnp.float32), 'key': jax.random.normal(ks[1], (B, S, DIM), jnp.float32), 'value': jax.random.normal(ks[2], (B, S, DIM), jnp.float32), 'Wq': jax.random.normal(ks[3], (DIM, DIM), jnp.float32) * w_scale, 'Wk': jax.random.normal(ks[4], (DIM, KV_DIM), jnp.float32) * w_scale, 'Wv': jax.random.normal(ks[5], (DIM, KV_DIM), jnp.float32) * w_scale, 'Wo': jax.random.normal(ks[6], (DIM, DIM), jnp.float32) * w_scale}
    _L2_xattn_all = _L2_xattn_setup()
    _L2_xattn_in = {k: v for k, v in _L2_xattn_all.items() if k in ('Wq', 'Wk', 'Wv', 'Wo')}
    del _L2_xattn_all

    def _L2_ffn_setup():
        import jax, jax.numpy as jnp
        import numpy as np
        TOP_K = 2
        key = jax.random.key(seed)
        k0, k1, k2 = jax.random.split(key, 3)
        B, S, D, H, E = (4, 256, 512, 512, 8)
        sc = 1.0 / np.sqrt(D).astype(np.float32)
        x = jax.random.normal(k0, (B, S, D), dtype=jnp.float32)
        W_gate = jax.random.normal(k1, (D, E), dtype=jnp.float32) * sc
        b_gate = jnp.zeros((E,), dtype=jnp.float32)
        W_e = jax.random.normal(k2, (E, D, H), dtype=jnp.float32) * sc
        b_e = jnp.zeros((E, H), dtype=jnp.float32)
        return {'x': x, 'W_gate': W_gate, 'b_gate': b_gate, 'W_e': W_e, 'b_e': b_e}
    _L2_ffn_all = _L2_ffn_setup()
    _L2_ffn_in = {k: v for k, v in _L2_ffn_all.items() if k in ('W_gate', 'b_gate', 'W_e', 'b_e')}
    del _L2_ffn_all

    def _L3_xattn_setup():
        import jax, jax.numpy as jnp
        import numpy as np
        NUM_HEADS = 32
        NUM_KV_HEADS = 8
        HEAD_DIM = 128
        HIDDEN = 512
        EPS = 1e-05

        def rmsnorm(x, w, eps=EPS):
            xf = x.astype(jnp.float32)
            var = jnp.mean(xf * xf, axis=-1, keepdims=True)
            return w * (xf * jax.lax.rsqrt(var + eps)).astype(x.dtype)
        key = jax.random.key(seed)
        ks = jax.random.split(key, 10)
        B, Q, KV = (1, 128, 6404)
        s = 1.0 / np.sqrt(HIDDEN)
        return {'hidden_states': jax.random.normal(ks[0], (B, Q, HIDDEN), jnp.float32), 'cross_attention_states': jax.random.normal(ks[1], (B, KV, HIDDEN), jnp.float32), 'attention_mask': jnp.zeros((B, 1, Q, KV), jnp.float32), 'q_proj_w': jax.random.normal(ks[2], (NUM_HEADS * HEAD_DIM, HIDDEN), jnp.float32) * s, 'k_proj_w': jax.random.normal(ks[3], (NUM_KV_HEADS * HEAD_DIM, HIDDEN), jnp.float32) * s, 'v_proj_w': jax.random.normal(ks[4], (NUM_KV_HEADS * HEAD_DIM, HIDDEN), jnp.float32) * s, 'o_proj_w': jax.random.normal(ks[5], (HIDDEN, NUM_HEADS * HEAD_DIM), jnp.float32) * s, 'q_norm_w': jnp.ones((HEAD_DIM,), jnp.float32), 'k_norm_w': jnp.ones((HEAD_DIM,), jnp.float32)}
    _L3_xattn_all = _L3_xattn_setup()
    _L3_xattn_in = {k: v for k, v in _L3_xattn_all.items() if k in ('q_proj_w', 'k_proj_w', 'v_proj_w', 'o_proj_w', 'q_norm_w', 'k_norm_w')}
    del _L3_xattn_all

    def _L3_ffn_setup():
        import jax, jax.numpy as jnp
        import numpy as np
        TOP_K = 2
        SCALING = 32.0 / 64.0
        key = jax.random.key(seed)
        ks = jax.random.split(key, 6)
        Bsz, S, Din, Dout, R, E = (4, 256, 512, 512, 64, 16)
        x = jax.random.normal(ks[0], (Bsz, S, Din), dtype=jnp.float32)
        base_w = jax.random.normal(ks[1], (Dout, Din), dtype=jnp.float32) * 0.02
        base_b = jax.random.normal(ks[2], (Dout,), dtype=jnp.float32) * 0.02
        A = jax.random.normal(ks[3], (R, Din), dtype=jnp.float32) * (1.0 / np.sqrt(Din))
        B = jax.random.normal(ks[4], (E, Dout, R), dtype=jnp.float32) * 0.02
        router_w = jax.random.normal(ks[5], (E, Din), dtype=jnp.float32) * 0.02
        return {'x': x, 'base_w': base_w, 'base_b': base_b, 'A': A, 'B': B, 'router_w': router_w}
    _L3_ffn_all = _L3_ffn_setup()
    _L3_ffn_in = {k: v for k, v in _L3_ffn_all.items() if k in ('base_w', 'base_b', 'A', 'B', 'router_w')}
    del _L3_ffn_all
    return {'x': x, 'ctx_4096': ctx_4096, 'itok_BxS2_0_2047': itok_BxS2_0_2047, 'mask_1x1xSxS2_ff0': mask_1x1xSxS2_ff0, 'L0_xattn_Wq': _L0_xattn_in['Wq'], 'L0_xattn_Wk': _L0_xattn_in['Wk'], 'L0_xattn_Wv': _L0_xattn_in['Wv'], 'L0_xattn_Wo': _L0_xattn_in['Wo'], 'L0_ffn_gate_t': _L0_ffn_in['gate_t'], 'L0_ffn_up_t': _L0_ffn_in['up_t'], 'L0_ffn_down_t': _L0_ffn_in['down_t'], 'L0_ffn_gate_s': _L0_ffn_in['gate_s'], 'L0_ffn_up_s': _L0_ffn_in['up_s'], 'L0_ffn_down_s': _L0_ffn_in['down_s'], 'L1_xattn_Wq': _L1_xattn_in['Wq'], 'L1_xattn_Wk': _L1_xattn_in['Wk'], 'L1_xattn_Wv': _L1_xattn_in['Wv'], 'L1_xattn_Wo': _L1_xattn_in['Wo'], 'L1_xattn_q_norm_w': _L1_xattn_in['q_norm_w'], 'L1_xattn_k_norm_w': _L1_xattn_in['k_norm_w'], 'L1_ffn_router_w': _L1_ffn_in['router_w'], 'L1_ffn_router_b': _L1_ffn_in['router_b'], 'L1_ffn_A': _L1_ffn_in['A'], 'L1_ffn_Bm': _L1_ffn_in['Bm'], 'L2_xattn_Wq': _L2_xattn_in['Wq'], 'L2_xattn_Wk': _L2_xattn_in['Wk'], 'L2_xattn_Wv': _L2_xattn_in['Wv'], 'L2_xattn_Wo': _L2_xattn_in['Wo'], 'L2_ffn_W_gate': _L2_ffn_in['W_gate'], 'L2_ffn_b_gate': _L2_ffn_in['b_gate'], 'L2_ffn_W_e': _L2_ffn_in['W_e'], 'L2_ffn_b_e': _L2_ffn_in['b_e'], 'L3_xattn_q_proj_w': _L3_xattn_in['q_proj_w'], 'L3_xattn_k_proj_w': _L3_xattn_in['k_proj_w'], 'L3_xattn_v_proj_w': _L3_xattn_in['v_proj_w'], 'L3_xattn_o_proj_w': _L3_xattn_in['o_proj_w'], 'L3_xattn_q_norm_w': _L3_xattn_in['q_norm_w'], 'L3_xattn_k_norm_w': _L3_xattn_in['k_norm_w'], 'L3_ffn_base_w': _L3_ffn_in['base_w'], 'L3_ffn_base_b': _L3_ffn_in['base_b'], 'L3_ffn_A': _L3_ffn_in['A'], 'L3_ffn_B': _L3_ffn_in['B'], 'L3_ffn_router_w': _L3_ffn_in['router_w']}

def reference(x, ctx_4096, itok_BxS2_0_2047, mask_1x1xSxS2_ff0, L0_xattn_Wq, L0_xattn_Wk, L0_xattn_Wv, L0_xattn_Wo, L0_ffn_gate_t, L0_ffn_up_t, L0_ffn_down_t, L0_ffn_gate_s, L0_ffn_up_s, L0_ffn_down_s, L1_xattn_Wq, L1_xattn_Wk, L1_xattn_Wv, L1_xattn_Wo, L1_xattn_q_norm_w, L1_xattn_k_norm_w, L1_ffn_router_w, L1_ffn_router_b, L1_ffn_A, L1_ffn_Bm, L2_xattn_Wq, L2_xattn_Wk, L2_xattn_Wv, L2_xattn_Wo, L2_ffn_W_gate, L2_ffn_b_gate, L2_ffn_W_e, L2_ffn_b_e, L3_xattn_q_proj_w, L3_xattn_k_proj_w, L3_xattn_v_proj_w, L3_xattn_o_proj_w, L3_xattn_q_norm_w, L3_xattn_k_norm_w, L3_ffn_base_w, L3_ffn_base_b, L3_ffn_A, L3_ffn_B, L3_ffn_router_w):
    import jax
    import jax.numpy as jnp

    def _L0_xattn_ref(query, key, value, position_ids, Wq, Wk, Wv, Wo):
        import jax, jax.numpy as jnp
        import numpy as np
        HIDDEN = 512
        N_HEADS = 32
        N_KV_HEADS = 8
        HEAD_DIM = HIDDEN // N_HEADS
        N_REP = N_HEADS // N_KV_HEADS
        ROPE_THETA = 10000.0
        B, S = (2, 256)

        def _rotate_half(x):
            x1, x2 = jnp.split(x, 2, axis=-1)
            return jnp.concatenate((-x2, x1), axis=-1)

        def _rope_cos_sin(position_ids):
            inv_freq = 1.0 / ROPE_THETA ** (jnp.arange(0, HEAD_DIM, 2, dtype=jnp.float32) / HEAD_DIM)
            freqs = position_ids[..., None].astype(jnp.float32) * inv_freq
            emb = jnp.concatenate((freqs, freqs), axis=-1)
            return (jnp.cos(emb)[:, None, :, :], jnp.sin(emb)[:, None, :, :])
        nb, q_len, _ = query.shape
        q = jnp.einsum('bse,ef->bsf', query, Wq).reshape(nb, q_len, N_HEADS, HEAD_DIM).transpose(0, 2, 1, 3)
        k = jnp.einsum('bse,ef->bsf', key, Wk).reshape(nb, q_len, N_KV_HEADS, HEAD_DIM).transpose(0, 2, 1, 3)
        v = jnp.einsum('bse,ef->bsf', value, Wv).reshape(nb, q_len, N_KV_HEADS, HEAD_DIM).transpose(0, 2, 1, 3)
        cos, sin = _rope_cos_sin(position_ids)
        q = q * cos + _rotate_half(q) * sin
        k = k * cos + _rotate_half(k) * sin
        k = jnp.repeat(k, N_REP, axis=1)
        v = jnp.repeat(v, N_REP, axis=1)
        scale = 1.0 / jnp.sqrt(jnp.asarray(HEAD_DIM, q.dtype))
        scores = jnp.einsum('bhqd,bhkd->bhqk', q, k) * scale
        probs = jax.nn.softmax(scores, axis=-1)
        ctx = jnp.einsum('bhqk,bhkd->bhqd', probs, v)
        ctx = ctx.transpose(0, 2, 1, 3).reshape(nb, q_len, N_HEADS * HEAD_DIM)
        return jnp.einsum('bsf,fe->bse', ctx, Wo)

    def _L0_ffn_ref(x, gate_t, up_t, down_t, gate_s, up_s, down_s):
        import jax, jax.numpy as jnp
        import numpy as np
        H, FF = (512, 1792)
        B, S = (4, 256)
        Bb, Ss, Hh = x.shape
        x_flat = x.reshape(Bb * Ss, Hh)
        gate_w = gate_t.astype(jnp.float32) * gate_s[:, None]
        up_w = up_t.astype(jnp.float32) * up_s[:, None]
        down_w = down_t.astype(jnp.float32) * down_s[:, None]
        gate_out = x_flat @ gate_w.T
        up_out = x_flat @ up_w.T
        hidden = jax.nn.silu(gate_out) * up_out
        out_flat = hidden @ down_w.T
        return out_flat.reshape(Bb, Ss, -1)

    def _L1_xattn_ref(latents, context, Wq, Wk, Wv, Wo, q_norm_w, k_norm_w):
        import jax, jax.numpy as jnp
        import numpy as np
        HEADS = 32
        KV_HEADS = 8
        HEAD_DIM = 128
        EPS = 1e-06

        def rms_norm(x, w):
            var = jnp.mean(jnp.square(x.astype(jnp.float32)), axis=-1, keepdims=True)
            return (x.astype(jnp.float32) * jax.lax.rsqrt(var + EPS)).astype(x.dtype) * w
        bsz, q_len, hidden = latents.shape
        kv = jnp.concatenate([context, latents], axis=1)
        kv_len = kv.shape[1]
        groups = HEADS // KV_HEADS
        q = (latents @ Wq).reshape(bsz, q_len, HEADS, HEAD_DIM).transpose(0, 2, 1, 3)
        k = (kv @ Wk).reshape(bsz, kv_len, KV_HEADS, HEAD_DIM).transpose(0, 2, 1, 3)
        v = (kv @ Wv).reshape(bsz, kv_len, KV_HEADS, HEAD_DIM).transpose(0, 2, 1, 3)
        q = rms_norm(q, q_norm_w)
        k = rms_norm(k, k_norm_w)
        qg = q.reshape(bsz, KV_HEADS, groups, q_len, HEAD_DIM)
        scale = 1.0 / np.sqrt(HEAD_DIM)
        scores = jnp.einsum('bhgqd,bhkd->bhgqk', qg, k) * scale
        probs = jax.nn.softmax(scores.astype(jnp.float32), axis=-1).astype(q.dtype)
        out = jnp.einsum('bhgqk,bhkd->bhgqd', probs, v)
        out = out.reshape(bsz, HEADS, q_len, HEAD_DIM).transpose(0, 2, 1, 3)
        out = out.reshape(bsz, q_len, HEADS * HEAD_DIM)
        return out @ Wo

    def _L1_ffn_ref(x, router_w, router_b, A, Bm):
        import jax, jax.numpy as jnp
        import numpy as np
        B_, S, D = (4, 512, 512)
        E, R, O = (8, 16, 512)
        TOP_K = 2
        SCALING = 8.0 / R
        flat = x.reshape(-1, x.shape[-1])
        N = flat.shape[0]
        logits = flat @ router_w.T + router_b
        probs = jax.nn.softmax(logits, axis=-1)
        topv, topi = jax.lax.top_k(probs, TOP_K)
        gates = topv / jnp.sum(topv, axis=-1, keepdims=True)
        w = jnp.zeros((N, E), dtype=flat.dtype).at[jnp.arange(N)[:, None], topi].add(gates)
        h = jnp.einsum('nd,erd->ner', flat, A)
        hw = h * w[:, :, None]
        out = jnp.einsum('ner,eor->no', hw, Bm) * SCALING
        return out.reshape(*x.shape[:-1], O)

    def _L2_xattn_ref(query, key, value, Wq, Wk, Wv, Wo):
        import jax, jax.numpy as jnp
        import numpy as np
        DIM = 512
        NUM_HEADS = 32
        NUM_KV_HEADS = 8
        HEAD_DIM = DIM // NUM_HEADS
        KV_DIM = DIM // (NUM_HEADS // NUM_KV_HEADS)
        B, S = (1, 256)
        b, sq, _ = query.shape
        _, sk, _ = key.shape
        rep = NUM_HEADS // NUM_KV_HEADS
        q = (query @ Wq).reshape(b, sq, NUM_HEADS, HEAD_DIM).transpose(0, 2, 1, 3)
        k = (key @ Wk).reshape(b, sk, NUM_KV_HEADS, HEAD_DIM).transpose(0, 2, 1, 3)
        v = (value @ Wv).reshape(b, sk, NUM_KV_HEADS, HEAD_DIM).transpose(0, 2, 1, 3)
        k = jnp.repeat(k, rep, axis=1)
        v = jnp.repeat(v, rep, axis=1)
        scale = HEAD_DIM ** (-0.5)
        scores = jnp.einsum('bhqd,bhkd->bhqk', q, k) * scale
        probs = jax.nn.softmax(scores, axis=-1)
        out = jnp.einsum('bhqk,bhkd->bhqd', probs, v)
        out = out.transpose(0, 2, 1, 3).reshape(b, sq, DIM)
        return out @ Wo

    def _L2_ffn_ref(x, W_gate, b_gate, W_e, b_e):
        import jax, jax.numpy as jnp
        import numpy as np
        TOP_K = 2
        logits = x @ W_gate + b_gate
        _, top_idx = jax.lax.top_k(logits, TOP_K)
        y_all = jax.nn.relu(jnp.einsum('bsd,edh->bseh', x, W_e) + b_e)
        y = jnp.take_along_axis(y_all, top_idx[..., None], axis=2)
        return y.mean(axis=2)

    def _L3_xattn_ref(hidden_states, cross_attention_states, attention_mask, q_proj_w, k_proj_w, v_proj_w, o_proj_w, q_norm_w, k_norm_w):
        import jax, jax.numpy as jnp
        import numpy as np
        NUM_HEADS = 32
        NUM_KV_HEADS = 8
        HEAD_DIM = 128
        HIDDEN = 512
        EPS = 1e-05

        def rmsnorm(x, w, eps=EPS):
            xf = x.astype(jnp.float32)
            var = jnp.mean(xf * xf, axis=-1, keepdims=True)
            return w * (xf * jax.lax.rsqrt(var + eps)).astype(x.dtype)
        B, Q, _ = hidden_states.shape
        KV = cross_attention_states.shape[1]
        n_rep = NUM_HEADS // NUM_KV_HEADS
        q = (hidden_states @ q_proj_w.T).reshape(B, Q, NUM_HEADS, HEAD_DIM).transpose(0, 2, 1, 3)
        k = (cross_attention_states @ k_proj_w.T).reshape(B, KV, NUM_KV_HEADS, HEAD_DIM).transpose(0, 2, 1, 3)
        v = (cross_attention_states @ v_proj_w.T).reshape(B, KV, NUM_KV_HEADS, HEAD_DIM).transpose(0, 2, 1, 3)
        q = rmsnorm(q, q_norm_w)
        k = jnp.repeat(k, n_rep, axis=1)
        v = jnp.repeat(v, n_rep, axis=1)
        k = rmsnorm(k, k_norm_w)
        scale = 1.0 / np.sqrt(HEAD_DIM)
        scores = jnp.einsum('bhqd,bhkd->bhqk', q, k) * scale + attention_mask
        attn = jax.nn.softmax(scores.astype(jnp.float32), axis=-1).astype(q.dtype)
        out = jnp.einsum('bhqk,bhkd->bhqd', attn, v)
        out = out.transpose(0, 2, 1, 3).reshape(B, Q, NUM_HEADS * HEAD_DIM)
        return out @ o_proj_w.T

    def _L3_ffn_ref(x, base_w, base_b, A, B, router_w):
        import jax, jax.numpy as jnp
        import numpy as np
        TOP_K = 2
        SCALING = 32.0 / 64.0
        base_out = jnp.einsum('bsi,oi->bso', x, base_w) + base_b
        res_hidden = jnp.einsum('bsi,ri->bsr', x, A)
        logits = jnp.einsum('bsi,ei->bse', x, router_w)
        probs = jax.nn.softmax(logits, axis=-1)
        topw, topi = jax.lax.top_k(probs, TOP_K)
        topw = topw / (jnp.sum(topw, axis=-1, keepdims=True) + 1e-06)
        num_experts = B.shape[0]
        combine = jnp.sum(jax.nn.one_hot(topi, num_experts, dtype=x.dtype) * topw[..., None], axis=-2)
        delta = jnp.einsum('bse,bsr,eor->bso', combine, res_hidden, B)
        return base_out + delta * SCALING
    x = x + _L0_xattn_ref(_layernorm(x, axis=-1), ctx_4096, ctx_4096, itok_BxS2_0_2047, L0_xattn_Wq, L0_xattn_Wk, L0_xattn_Wv, L0_xattn_Wo)
    x = x + _L0_ffn_ref(_layernorm(x, axis=-1), L0_ffn_gate_t, L0_ffn_up_t, L0_ffn_down_t, L0_ffn_gate_s, L0_ffn_up_s, L0_ffn_down_s)
    x = x + _L1_xattn_ref(_layernorm(x, axis=-1), ctx_4096, L1_xattn_Wq, L1_xattn_Wk, L1_xattn_Wv, L1_xattn_Wo, L1_xattn_q_norm_w, L1_xattn_k_norm_w)
    x = x + _L1_ffn_ref(_layernorm(x, axis=-1), L1_ffn_router_w, L1_ffn_router_b, L1_ffn_A, L1_ffn_Bm)
    x = x + _L2_xattn_ref(_layernorm(x, axis=-1), ctx_4096, ctx_4096, L2_xattn_Wq, L2_xattn_Wk, L2_xattn_Wv, L2_xattn_Wo)
    x = x + _L2_ffn_ref(_layernorm(x, axis=-1), L2_ffn_W_gate, L2_ffn_b_gate, L2_ffn_W_e, L2_ffn_b_e)
    x = x + _L3_xattn_ref(_layernorm(x, axis=-1), ctx_4096, mask_1x1xSxS2_ff0, L3_xattn_q_proj_w, L3_xattn_k_proj_w, L3_xattn_v_proj_w, L3_xattn_o_proj_w, L3_xattn_q_norm_w, L3_xattn_k_norm_w)
    x = x + _L3_ffn_ref(_layernorm(x, axis=-1), L3_ffn_base_w, L3_ffn_base_b, L3_ffn_A, L3_ffn_B, L3_ffn_router_w)
    return x

_drawn_inputs = setup_inputs


def setup_inputs(seed=0):
    import zlib

    import numpy as np

    out = dict(_drawn_inputs(seed))
    spreads = {'L1_xattn_q_norm_w': (1.0, 0.6),
     'L1_xattn_k_norm_w': (1.0, 0.6),
     'L2_ffn_b_gate': (0.0, 0.1),
     'L2_ffn_b_e': (0.0, 0.411),
     'L3_xattn_q_norm_w': (1.0, 0.2),
     'L3_xattn_k_norm_w': (1.0, 0.2)}
    factors = {'L1_ffn_router_w': 3.541,
     'L1_ffn_router_b': 188.027,
     'L1_ffn_A': 2.776,
     'L3_ffn_base_b': 7.75,
     'L3_ffn_A': 2.673,
     'L3_ffn_B': 2.74,
     'L3_ffn_router_w': 2.877}
    for name, (base, spread) in spreads.items():
        noise = np.random.default_rng([zlib.crc32(name.encode()), seed]).standard_normal(out[name].shape)
        drawn = base * np.exp(spread * noise) if base else spread * noise
        out[name] = jnp.asarray(drawn.astype(out[name].dtype))
    for name, factor in factors.items():
        out[name] = (out[name] * factor).astype(out[name].dtype)
    return out
```

```python
from contextlib import ExitStack

import numpy as np
import concourse.bass as bass
from concourse import mybir

F32 = mybir.dt.float32
F16 = mybir.dt.float16
I32 = mybir.dt.int32
U32 = mybir.dt.uint32
ALU = mybir.AluOpType
ACT = mybir.ActivationFunctionType
AXX = mybir.AxisListType.X

P = 128
B = 8
S = 128
T = B * S
D = 512
DC = D // P
G = 8
HPG = 4
ND = 16
FF = 1792
FC = FF // P
FP = FC // 2
UNITS = B * G
WSCALE = 64.0
UNSCALE = 1.0 / WSCALE
QKV = DC * (HPG * P) + DC * 2 * P
WOUT = HPG * D
NORM_EPS = 1e-5
LOG_EXP = "natural_log_exp_and_others"
ROPE_THETA = 10000.0
TWO_PI_HI = 6.28125
TWO_PI_MID = float((np.array([2 * np.pi - 6.28125], np.float32).view(np.uint32) & np.uint32(0xFFFFF000)).view(np.float32)[0])
TWO_PI_LO = float(2 * np.pi - 6.28125 - TWO_PI_MID)
ROUND = 1.5 * 2.0 ** 23

COLS = {}
_at = 0
for _name, _n in (("ident", P), ("head_of_row", HPG), ("iota", 16), ("gate_s", FC), ("up_s", FC),
                  ("down_s", D), ("q1", 1), ("k1", 1), ("q3", 1), ("k3", 1), ("router1_b", 8),
                  ("router2_b", 8), ("base_b", D), ("mask", S)):
    COLS[_name] = (_at, _at + _n)
    _at += _n
NCONST = _at


def weight_items():
    items, qkv, out = [], 0, 0

    def a(name, i, n, scaled=True):
        nonlocal qkv
        items.append((name, i, n, "qkv", qkv, scaled))
        qkv += 1

    def o(name, i, n):
        nonlocal out
        items.append((name, i, n, "out", out, True))
        out += 1

    a("w_qkv0", 0, QKV)
    o("w_out0", 0, WOUT)
    for j in range(FP):
        a("w_ffn0", j, QKV, False)
    for g in range(G):
        a("w_qkv1", g, QKV)
        o("w_out1", g, WOUT)
    a("w_ffn1", 0, 544 + 512)
    a("w_qkv2", 0, QKV)
    o("w_out2", 0, WOUT)
    for e in range(8):
        a("w_ffn2", e, 2048)
    for g in range(G):
        a("w_qkv3", g, QKV)
        o("w_out3", g, WOUT)
    a("w_ffn3a", 0, 2048 + 320)
    o("w_ffn3b", 0, 2048)
    o("w_ffn3b", 1, 2048)
    return items


ITEMS = weight_items()
NUMBER = {(name, i): k for k, (name, i, *_rest) in enumerate(ITEMS)}


def build(nc, ins, out, phases=8):
    ctx = ExitStack()
    with ctx:
        def sb(name, shape, dt):
            return ctx.enter_context(nc.sbuf_tensor(name, [P] + shape, dt))

        def sem(name):
            return ctx.enter_context(nc.semaphore(name))

        x = sb("x", [B, D], F32)
        xn = sb("xn", [2, D], F32)
        xnT_hi, xnT_lo = sb("xnT_hi", [DC, T], F16), sb("xnT_lo", [DC, T], F16)
        ctxT_hi, ctxT_lo = sb("ctxT_hi", [DC, T], F16), sb("ctxT_lo", [DC, T], F16)
        const = sb("const", [NCONST], F32)
        expert_b = sb("expert_b", [8, D], F32)
        wgate2 = sb("wgate2", [DC * 8], F32)
        wgate2_hi, wgate2_lo = sb("wgate2_hi", [DC * 8], F16), sb("wgate2_lo", [DC * 8], F16)
        pos = sb("pos", [B], I32)
        raw = sb("raw", [2, QKV], F32)
        wa_hi, wa_lo = sb("wa_hi", [2, QKV], F16), sb("wa_lo", [2, QKV], F16)
        wo_hi, wo_lo = sb("wo_hi", [2, WOUT], F16), sb("wo_lo", [2, WOUT], F16)
        stats = sb("stats", [B, 6], F32)
        mv = sb("mv", [B, 2], F32)
        ln_log, ln_r0, ln_t, ln_r = (sb(n, [B], F32) for n in ("ln_log", "ln_r0", "ln_t", "ln_r"))
        ln_a = sb("ln_a", [B], F32)
        qn = sb("qn", [D], F32)
        kn = sb("kn", [D], F32)
        probs = sb("probs", [2, HPG * 2 * S], F32)
        pT_hi, pT_lo = sb("pT_hi", [2, HPG * S], F16), sb("pT_lo", [2, HPG * S], F16)
        v_hi, v_lo = sb("v_hi", [2, 2 * P], F16), sb("v_lo", [2, 2 * P], F16)
        qT_hi, qT_lo = sb("qT_hi", [2, HPG * S], F16), sb("qT_lo", [2, HPG * S], F16)
        kT_hi, kT_lo = sb("kT_hi", [4 * S], F16), sb("kT_lo", [4 * S], F16)
        oT_hi, oT_lo = sb("oT_hi", [HPG * S], F16), sb("oT_lo", [HPG * S], F16)
        negmax = sb("negmax", [2, HPG], F32)
        squares = sb("squares", [6 * P], F32)
        sumsq = sb("sumsq", [6], F32)
        rms_log, rms_r0, rms_t, rms_a, rms_r = (sb(n, [6], F32) for n in ("rms_log", "rms_r0", "rms_t", "rms_a", "rms_r"))
        total = sb("total", [2, HPG], F32)
        inv_total = sb("inv_total", [2, HPG], F32)
        w_comb = sb("w_comb", [2], F32)
        masked = sb("masked", [HPG * S], F32)
        bd_hi, bd_lo = sb("bd_hi", [2, 4 * HPG * S], F16), sb("bd_lo", [2, 4 * HPG * S], F16)
        ctx_raw = [t[:, :, :].rearrange("p a b -> p (a b)").bitcast(F32) for t in (bd_hi, bd_lo)]
        rope_ab = sb("rope_ab", [2, D], F32)
        rope_a, rope_b = rope_ab[:, 0, :], rope_ab[:, 1, :]
        ropek_a, ropek_b = sb("ropek_a", [P], F32), sb("ropek_b", [P], F32)
        posf = sb("posf", [B], F32)
        angle, turns, red = (sb(n, [B, 2, 8], F32) for n in ("angle", "turns", "red"))
        trig = sb("trig", [B, 2, 8], F32)
        cosw, sinw = sb("cosw", [B, ND], F32), sb("sinw", [B, ND], F32)
        total_n = sb("total_n", [2, 32], F32)
        inv_total_n = sb("inv_total_n", [32], F32)
        on = masked
        silu = rope_ab
        hid = sb("hid", [2, D], F32)
        hid_hi, hid_lo = (t[:, :, :].rearrange("p s (c t) -> p s c t", c=2) for t in (bd_hi, bd_lo))
        ytmp = sb("ytmp", [2, D], F32)
        logits = sb("logits", [B, 16], F32)
        expl = sb("expl", [B, 16], F32)
        rprob = sb("rprob", [B, 16], F32)
        rmax, rsum, rinv = sb("rmax", [B], F32), sb("rsum", [B], F32), sb("rinv", [B], F32)
        top = sb("top", [B, 8], F32)
        topi = sb("topi", [B, 8], U32)
        topf = sb("topf", [B, 8], F32)
        gsum, ginv = sb("gsum", [B], F32), sb("ginv", [B], F32)
        gates = sb("gates", [B, 2], F32)
        pick_a, pick_b, route = sb("pick_a", [B, 16], F32), sb("pick_b", [B, 16], F32), sb("route", [B, 16], F32)
        down = hid[:, :, :].rearrange("p s (c r) -> p (s c) r", r=P)
        mixed = probs
        mixT_hi, mixT_lo = (t[:, :, :].rearrange("p a b -> p (a b)") for t in (pT_hi, pT_lo))

        bank = [ctx.enter_context(nc.psum_tensor(f"bank{i}", [P, 512], F32)) for i in range(8)]
        Q, KV, S0, S1, PT0, PT1, O, Y = range(8)

        def c(name):
            a, b = COLS[name]
            return const[:, a:b]

        ident = c("ident")

        x_loaded, const_loaded, expert_b_loaded, pos_loaded, wgate2_loaded = (
            sem(n) for n in ("x_loaded", "const_loaded", "expert_b_loaded", "pos_loaded", "wgate2_loaded"))
        ctx_loaded = [sem(f"ctx_loaded{i}") for i in range(2)]
        raw_loaded = [sem(f"raw_loaded{i}") for i in range(2)]
        hi_split, split_done = sem("hi_split"), sem("split_done")
        ctx_hi_split, ctx_split, wgate2_split = sem("ctx_hi_split"), sem("ctx_split"), sem("wgate2_split")
        qkv_used, out_used = sem("qkv_used"), sem("out_used")
        w_comb_ready = sem("w_comb_ready")
        ln_aggr, ln_est, ln_act, ln_newton, ln_norm, ln_T, ln_hi, ln_lo = (
            sem(n) for n in ("ln_aggr", "ln_est", "ln_act", "ln_newton", "ln_norm", "ln_T", "ln_hi", "ln_lo"))
        (w_proj, w_qkT, w_scores, w_probsT, w_attn, w_out) = (
            sem("w_" + n) for n in ("proj", "qkT", "scores", "probsT", "attn", "outp"))
        (w_exp, w_sumsq, w_log, w_rms0, w_vhi, w_phi, w_qkhi, w_ohi) = (
            sem("w_" + n) for n in ("exp", "sumsq", "log", "rms0", "vhi", "phi", "qkhi", "ohi"))
        (w_masked, w_max, w_inv, w_pnorm, w_newton, w_qknorm, w_vlo, w_plo, w_qklo, w_olo, w_y) = (
            sem("w_" + n) for n in ("masked", "max", "inv", "pnorm", "newton", "qknorm", "vlo", "plo", "qklo",
                                    "olo", "y"))
        (nb_proj, nb_qkT, nb_oT, nb_out) = (sem("nb_" + n) for n in ("proj", "qkT", "oT", "outp"))
        (ng_scores, ng_probsT, ng_attn) = (sem("ng_" + n) for n in ("scores", "probsT", "attn"))
        (nb_vhi, nb_qcopy, nb_qhi, nb_khi, nb_ohi, ng_exp, ng_phi) = (
            sem(n) for n in ("nb_vhi", "nb_qcopy", "nb_qhi", "nb_khi", "nb_ohi", "ng_exp", "ng_phi"))
        (nb_vlo, nb_rope, nb_qk, nb_qlo, nb_klo, nb_bd, nb_inv, nb_on, nb_olo, nb_y, ng_max, ng_plo) = (
            sem(n) for n in ("nb_vlo", "nb_rope", "nb_qk", "nb_qlo", "nb_klo", "nb_bd", "nb_inv", "nb_on", "nb_olo",
                             "nb_y", "ng_max", "ng_plo"))
        angles, sines = sem("angles"), sem("sines")
        f0_gu, f0_y, f0_silu, f0_hid, f0_split, f0_scaled, f0_add = (
            sem("f0_" + n) for n in ("gu", "y", "silu", "hid", "split", "scaled", "add"))
        f0_split_hi = sem("f0_split_hi")
        rt_z, rt_copy, rt_step, rt_exp, rt_done = (sem("rt_" + n) for n in ("z", "copy", "step", "exp", "done"))
        mx_mixed, mx_T, mx_hi, mx_lo, mx_y, mx_add, mx_tmp = (
            sem("mx_" + n) for n in ("mixed", "T", "hi", "lo", "y", "add", "tmp"))
        e_y, e_tmp, e_relu, e_add = (sem("e_" + n) for n in ("y", "tmp", "relu", "add"))
        stored = sem("stored")

        block = ctx.enter_context(nc.Block())
        n_items = {1: 2, 2: 2 + FP, 3: 2 + FP + 16, 4: 2 + FP + 17, 5: 2 + FP + 19, 6: 2 + FP + 27,
                   7: 2 + FP + 43, 8: len(ITEMS)}[phases]

        final = {1: (nb_y, 8), 2: (f0_add, 56), 3: (w_y, 64), 4: (mx_add, 8), 5: (nb_y, 16), 6: (e_add, 64),
                 7: (w_y, 128), 8: (mx_add, 16)}[phases]

        @block.sync
        def _(sp):
            sp.dma_start(x[:, :, :], ins["x"]).then_inc(x_loaded, 16)
            sp.dma_start(pos[:, :], ins["pos"]).then_inc(pos_loaded, 16)
            sp.dma_start(raw[:, 0, :], ins["w_qkv0"][0]).then_inc(raw_loaded[0], 16)
            sp.dma_start(const[:, :], ins["const"]).then_inc(const_loaded, 16)

            def load(k, name, i):
                dst = raw[:, k % 2, 0:ITEMS[k][2]]
                if not ITEMS[k][5]:
                    dst = dst.bitcast(I32)
                sp.dma_start(dst, ins[name][i]).then_inc(raw_loaded[k % 2], 16)

            for h in range(2):
                sp.dma_start(ctx_raw[h], ins["ctxT"][h]).then_inc(ctx_loaded[h], 16)
            for k, (name, i, n, _, _, _) in enumerate(ITEMS[:n_items]):
                if k == 0:
                    continue
                if k >= 2:
                    sp.wait_ge(split_done, k - 1)
                load(k, name, i)
                if k == 2:
                    sp.dma_start(expert_b[:, :, :], ins["expert_b"]).then_inc(expert_b_loaded, 16)
                    sp.dma_start(wgate2[:, :], ins["wgate2"]).then_inc(wgate2_loaded, 16)
            sp.wait_ge(final[0], final[1])
            sp.dma_start(out, x[:, :, :]).then_inc(stored, 16)
            sp.wait_ge(stored, 16)

        @block.gpsimd
        def _(pool):
            def item(k):
                name, i, n, kind, slot, scaled = ITEMS[k]
                pool.wait_ge(raw_loaded[k % 2], 16 * (k // 2 + 1))
                if slot >= 2:
                    pool.wait_ge(qkv_used if kind == "qkv" else out_used, slot - 1)
                hi, lo = (wa_hi, wa_lo) if kind == "qkv" else (wo_hi, wo_lo)
                hi, lo = hi[:, slot % 2, 0:n], lo[:, slot % 2, 0:n]
                src = raw[:, k % 2, 0:n]
                landed, scale = (src, WSCALE) if scaled else (src.bitcast(I32), 1.0)
                pool.tensor_scalar(hi, landed, scale, 1.0, ALU.mult, ALU.mult)
                pool.tensor_scalar(src, landed, scale, 1.0, ALU.mult, ALU.mult).then_inc(hi_split, 1)
                pool.wait_ge(hi_split, k + 1)
                pool.tensor_tensor(lo, src, hi, ALU.subtract).then_inc(split_done, 1)

            def keys(n, b):
                BB = n * B + b
                pool.wait_ge(nb_klo, BB + 1)
                if b >= 2:
                    pool.wait_ge(ng_scores, (BB - 1) * G)
                for part, (dst, src) in enumerate(((bd_hi, kT_hi), (bd_lo, kT_lo))):
                    dv = dst[:, b % 2, :].rearrange("p (c h t) -> p c h t", c=4, h=HPG)
                    for h in range(HPG):
                        ins_ = pool.tensor_scalar(dv[:, :, h, :], src[:, :].rearrange("p (c t) -> p c t", c=4),
                                                  c("head_of_row")[:, h:h + 1], 1.0, ALU.mult, ALU.mult)
                ins_.then_inc(nb_bd, 1)

            def items(name, idx):
                for i in idx:
                    if NUMBER[name, i] < n_items:
                        item(NUMBER[name, i])

            item(0)
            item(1)
            if phases > 1:
                item(2)
            for b in range(B):
                keys(0, b)
            if phases > 1:
                for k in range(3, NUMBER["w_ffn2", 1]):
                    if k < n_items:
                        item(k)
            if phases > 4:
                pool.wait_ge(wgate2_loaded, 16)
                pool.tensor_scalar(wgate2_hi[:, :], wgate2[:, :], WSCALE, 1.0, ALU.mult, ALU.mult)
                pool.tensor_scalar(wgate2[:, :], wgate2[:, :], WSCALE, 1.0, ALU.mult, ALU.mult).then_inc(wgate2_split, 1)
                pool.wait_ge(wgate2_split, 1)
                pool.tensor_tensor(wgate2_lo[:, :], wgate2[:, :], wgate2_hi[:, :], ALU.subtract).then_inc(wgate2_split, 1)
                for b in range(B):
                    keys(1, b)
            for k in range(NUMBER["w_ffn2", 1], n_items):
                item(k)

        @block.tensor
        def _(pe):
            def passes(dst, pairs, start=True, stop=True):
                n = 3 * len(pairs)
                k = 0
                for lh, ll, rh, rl in pairs:
                    for l, r in ((lh, rh), (lh, rl), (ll, rh)):
                        mm = pe.matmul(dst, l, r, start=start and k == 0, stop=stop and k == n - 1)
                        k += 1
                return mm

            def tok(b):
                return slice(b * S, (b + 1) * S)

            def normed(n):
                for b in range(B):
                    pe.wait_ge(ln_norm, n * B + b + 1)
                    if b >= 4:
                        pe.wait_ge(ln_lo, n * B + b - 3)
                    for k in range(DC):
                        mm = pe.transpose(bank[4 + b % 4][:, k * P:(k + 1) * P], xn[:, b % 2, k * P:(k + 1) * P], ident)
                    mm.then_inc(ln_T, 1)

            def weights(name, i):
                pe.wait_ge(split_done, NUMBER[name, i] + 1)

            def narrow(n, name):
                slot_a, slot_o = ITEMS[NUMBER["w_qkv" + name, 0]][4] % 2, ITEMS[NUMBER["w_out" + name, 0]][4] % 2
                wqh = wa_hi[:, slot_a, 0:2048].rearrange("p (c n) -> p c n", c=DC)
                wql = wa_lo[:, slot_a, 0:2048].rearrange("p (c n) -> p c n", c=DC)
                wkh = wa_hi[:, slot_a, 2048:QKV].rearrange("p (c n) -> p c n", c=DC)
                wkl = wa_lo[:, slot_a, 2048:QKV].rearrange("p (c n) -> p c n", c=DC)

                def proj(b):
                    pe.wait_ge(ln_lo, 2 * n * 2 * B + b + 1)
                    if b:
                        pe.wait_ge(nb_qlo, n * B + b)
                        pe.wait_ge(nb_klo, n * B + b)
                    passes(bank[Q][:, :], [(xnT_hi[:, k, tok(b)], xnT_lo[:, k, tok(b)], wqh[:, k, :], wql[:, k, :])
                                           for k in range(DC)])
                    mm = passes(bank[KV][:, 0:256], [(ctxT_hi[:, k, tok(b)], ctxT_lo[:, k, tok(b)], wkh[:, k, :],
                                                      wkl[:, k, :]) for k in range(DC)])
                    mm.then_inc(nb_proj, 1)
                    if b == B - 1:
                        pe.wait_ge(nb_proj, (n + 1) * B)
                        pe.sem_inc(qkv_used, 1)

                def turn(b):
                    pe.wait_ge(nb_qk, n * B + b + 1)
                    if n == 1:
                        pe.wait_ge(nb_qcopy, b + 1)
                    pe.wait_ge(nb_vlo, n * B + b + 1)
                    for k in range(4):
                        pe.transpose(bank[Q][:, k * P:(k + 1) * P], qn[:, k * P:(k + 1) * P], ident)
                    for k in range(4):
                        mm = pe.transpose(bank[KV][:, k * P:(k + 1) * P], kn[:, k * P:(k + 1) * P], ident)
                    mm.then_inc(nb_qkT, 1)

                def scores(j):
                    b, g = divmod(j, G)
                    J = n * UNITS + j
                    if g == 0:
                        pe.wait_ge(nb_bd, n * B + b + 1)
                        pe.wait_ge(nb_qlo, n * B + b + 1)
                    if j >= 2:
                        pe.wait_ge(ng_exp, J - 1)
                    ch, m = divmod(g, 2)
                    rows = slice(64 * m, 64 * m + 64)
                    k0 = ch * HPG * S
                    mm = passes(bank[S0 + j % 2][:, :], [(qT_hi[rows, b % 2, ch * P:(ch + 1) * P],
                                                          qT_lo[rows, b % 2, ch * P:(ch + 1) * P],
                                                          bd_hi[rows, b % 2, k0:k0 + 512],
                                                          bd_lo[rows, b % 2, k0:k0 + 512])])
                    mm.then_inc(ng_scores, 1)

                def probs_T(j):
                    J = n * UNITS + j
                    pe.wait_ge(ng_exp, J + 1)
                    if j >= 2:
                        pe.wait_ge(ng_plo, J - 1)
                    for h in range(HPG):
                        mm = pe.transpose(bank[PT0 + j % 2][:, h * S:(h + 1) * S],
                                          probs[:, j % 2, h * S:(h + 1) * S], ident)
                    mm.then_inc(ng_probsT, 1)

                def attend(j):
                    b, g = divmod(j, G)
                    J = n * UNITS + j
                    pe.wait_ge(ng_plo, J + 1)
                    if g == 0:
                        pe.wait_ge(nb_vlo, n * B + b + 1)
                        if b >= 2:
                            pe.wait_ge(nb_y, n * B + b - 1)
                    for h in range(HPG):
                        o = bank[O + b % 2][:, (g * HPG + h) * ND:(g * HPG + h + 1) * ND]
                        vh, vl = v_hi[:, b % 2, g * ND:(g + 1) * ND], v_lo[:, b % 2, g * ND:(g + 1) * ND]
                        mm = passes(o, [(pT_hi[:, j % 2, h * S:(h + 1) * S], pT_lo[:, j % 2, h * S:(h + 1) * S], vh, vl)])
                    mm.then_inc(ng_attn, 1)

                def out_T(b):
                    pe.wait_ge(nb_on, n * B + b + 1)
                    for k in range(4):
                        mm = pe.transpose(bank[O + b % 2][:, k * P:(k + 1) * P], on[:, k * P:(k + 1) * P], ident)
                    mm.then_inc(nb_oT, 1)

                def out_proj(b):
                    pe.wait_ge(nb_olo, n * B + b + 1)
                    if b == 0:
                        weights("w_out" + name, 0)
                    wh = wo_hi[:, slot_o, :].rearrange("p (c n) -> p c n", c=DC)
                    wl = wo_lo[:, slot_o, :].rearrange("p (c n) -> p c n", c=DC)
                    mm = passes(bank[O + b % 2][:, :], [(oT_hi[:, k * P:(k + 1) * P], oT_lo[:, k * P:(k + 1) * P],
                                                         wh[:, k, :], wl[:, k, :]) for k in range(4)])
                    mm.then_inc(nb_out, 1)
                    if b == B - 1:
                        pe.wait_ge(nb_out, (n + 1) * B)
                        pe.sem_inc(out_used, 1)

                if n == 0:
                    pe.wait_ge(ctx_split, 2)
                weights("w_qkv" + name, 0)
                proj(0)
                turn(0)
                for j in range(UNITS + 8):
                    b, g = divmod(j, G)
                    if g == 0 and b + 1 < B:
                        proj(b + 1)
                    if j < UNITS:
                        scores(j)
                    if 1 <= j <= UNITS:
                        probs_T(j - 1)
                    if 2 <= j <= UNITS + 1:
                        attend(j - 2)
                    if g == 3 and b + 1 < B:
                        turn(b + 1)
                    if g == 4 and b >= 1:
                        out_T(b - 1)
                    if g == 6 and b >= 1:
                        out_proj(b - 1)

            def ffn0():
                def gate_up(v):
                    j, ch, hf = v // 4, v // 2 % 2, v % 2
                    slot = ITEMS[NUMBER["w_ffn0", j]][4] % 2
                    if v % 4 == 0:
                        weights("w_ffn0", j)
                    if v >= 2:
                        pe.wait_ge(f0_hid, v - 1)
                    for part, at in ((0, 0), (1, 1024)):
                        a = at + ch * 512
                        mm = passes(bank[2 * (v % 2) + part][:, :],
                                    [(wa_hi[:, slot, a + k * P:a + (k + 1) * P], wa_lo[:, slot, a + k * P:a + (k + 1) * P],
                                      xnT_hi[:, k, hf * 512:(hf + 1) * 512], xnT_lo[:, k, hf * 512:(hf + 1) * 512])
                                     for k in range(DC)])
                    mm.then_inc(f0_gu, 1)

                def down_proj(j, b):
                    slot = ITEMS[NUMBER["w_ffn0", j]][4] % 2
                    r = j * B + b
                    if b % 4 == 0:
                        pe.wait_ge(f0_split, 4 * j + 3 + b // 4)
                    if r >= 4:
                        pe.wait_ge(f0_scaled, r - 3)
                    mm = passes(bank[4 + r % 4][:, :],
                                [(hid_hi[:, j % 2, ch, tok(b)], hid_lo[:, j % 2, ch, tok(b)],
                                  wa_hi[:, slot, 2048 + ch * 512:2048 + (ch + 1) * 512],
                                  wa_lo[:, slot, 2048 + ch * 512:2048 + (ch + 1) * 512]) for ch in range(2)])
                    mm.then_inc(f0_y, 1)
                    if b == B - 1:
                        pe.wait_ge(f0_y, r + 1)
                        pe.sem_inc(qkv_used, 1)

                pe.wait_ge(ln_lo, 2 * B)
                for v in range(4 * FP + 4):
                    if v < 4 * FP:
                        gate_up(v)
                    if v >= 4:
                        down_proj(v // 4 - 1, 2 * (v % 4))
                        down_proj(v // 4 - 1, 2 * (v % 4) + 1)

            def wide(n, ln, name, tiles):
                base = n * UNITS
                par_a, par_o = ITEMS[NUMBER["w_qkv" + name, 0]][4] % 2, ITEMS[NUMBER["w_out" + name, 0]][4] % 2

                def project(U, r, first):
                    b, sl = r % B, (par_a + r // B) % 2
                    wqh = wa_hi[:, sl, 0:2048].rearrange("p (c n) -> p c n", c=DC)
                    wql = wa_lo[:, sl, 0:2048].rearrange("p (c n) -> p c n", c=DC)
                    wkh = wa_hi[:, sl, 2048:QKV].rearrange("p (c n) -> p c n", c=DC)
                    wkl = wa_lo[:, sl, 2048:QKV].rearrange("p (c n) -> p c n", c=DC)
                    if not first:
                        pe.wait_ge(w_qknorm, U)
                        pe.wait_ge(w_vlo, U)
                    passes(bank[Q][:, :], [(xnT_hi[:, k, tok(b)], xnT_lo[:, k, tok(b)], wqh[:, k, :], wql[:, k, :])
                                           for k in range(DC)])
                    for j in range(tiles):
                        sh, sl_ = (ctxT_hi, ctxT_lo) if j == 0 else (xnT_hi, xnT_lo)
                        mm = passes(bank[KV][:, j * 256:(j + 1) * 256],
                                    [(sh[:, k, tok(b)], sl_[:, k, tok(b)], wkh[:, k, :], wkl[:, k, :]) for k in range(DC)])
                    mm.then_inc(w_proj, 1)

                def turn(U, first):
                    pe.wait_ge(w_qknorm, U + 1)
                    if not first:
                        pe.wait_ge(w_exp, U)
                    for k in range(4):
                        pe.transpose(bank[S0][:, k * P:(k + 1) * P], qn[:, k * P:(k + 1) * P], ident)
                    for j in range(tiles):
                        mm = pe.transpose(bank[S1][:, j * P:(j + 1) * P], kn[:, j * P:(j + 1) * P], ident)
                    mm.then_inc(w_qkT, 1)

                def scores(U):
                    pe.wait_ge(w_qklo, U + 1)
                    width = tiles * S
                    for h in range(HPG):
                        bk, at = divmod(h * width, 512)
                        mm = passes(bank[S0 + bk][:, at:at + width],
                                    [(qT_hi[:, 0, h * S:(h + 1) * S], qT_lo[:, 0, h * S:(h + 1) * S],
                                      kT_hi[:, 0:width], kT_lo[:, 0:width])])
                    mm.then_inc(w_scores, 1)

                def probs_T(U, par, first):
                    pe.wait_ge(w_pnorm, U + 1)
                    if not first:
                        pe.wait_ge(w_plo, U)
                    pv = probs[:, par, 0:HPG * tiles * S].rearrange("p (h j t) -> p h j t", h=HPG, j=tiles)
                    for j in range(tiles):
                        for h in range(HPG):
                            mm = pe.transpose(bank[PT0 + j][:, h * S:(h + 1) * S], pv[:, h, j, :], ident)
                    mm.then_inc(w_probsT, 1)

                def attend(U, par, first):
                    pe.wait_ge(w_plo, U + 1)
                    pe.wait_ge(w_vlo, U + 1)
                    if not first:
                        pe.wait_ge(w_olo, U)
                    mm = passes(bank[O][:, :], [(v_hi[:, par, j * P:(j + 1) * P], v_lo[:, par, j * P:(j + 1) * P],
                                                 pT_hi[:, j, :], pT_lo[:, j, :]) for j in range(tiles)])
                    mm.then_inc(w_attn, 1)

                def out_proj(U, r, first):
                    sl = (par_o + r // B) % 2
                    pe.wait_ge(w_olo, U + 1)
                    if not first:
                        pe.wait_ge(w_y, U)
                    wh = wo_hi[:, sl, :].rearrange("p (c n) -> p c n", c=DC)
                    wl = wo_lo[:, sl, :].rearrange("p (c n) -> p c n", c=DC)
                    mm = passes(bank[Y][:, :], [(oT_hi[:, h * S:(h + 1) * S], oT_lo[:, h * S:(h + 1) * S],
                                                 wh[:, h, :], wl[:, h, :]) for h in range(HPG)])
                    mm.then_inc(w_out, 1)

                k0 = NUMBER["w_qkv" + name, 0]

                def step(i, r, seen, last=UNITS):
                    U = i * 16 + (base + r)
                    if seen < last:
                        if r % B == 0:
                            pe.wait_ge(split_done, i * 4 + (k0 + 2 * (r // B) + 1))
                        if seen < B:
                            pe.wait_ge(ln_lo, (ln + 1) * B if seen else ln * B + B)
                        project(U, r, seen == 0)
                        if r % B == B - 1:
                            pe.wait_ge(w_proj, U + 1)
                            pe.sem_inc(qkv_used, 1)
                    if 1 <= seen <= last:
                        probs_T(U - 1, (r - 1) % 2, seen == 1)
                    if seen >= 2:
                        if (r - 2) % B == 0:
                            pe.wait_ge(split_done, i * 4 + (k0 + 2 * ((r - 2) // B) + 2))
                        out_proj(U - 2, r - 2 if r >= 2 else r + 14, seen == 2)
                        if (r - 2) % B == B - 1:
                            pe.wait_ge(w_out, U - 1)
                            pe.sem_inc(out_used, 1)
                    if seen < last:
                        turn(U, seen == 0)
                    if 1 <= seen <= last:
                        attend(U - 1, (r - 1) % 2, seen == 1)
                    if seen < last:
                        scores(U)

                for r in range(16):
                    step(0, r, r)
                with pe.Fori(1, UNITS // 16) as i:
                    for r in range(16):
                        step(i, r, 16)
                for r in range(2):
                    step(UNITS // 16, r, UNITS + r)

            def router(n, wh, wl, cols, at=0):
                for b in range(B):
                    mm = passes(bank[b][:, 0:cols], [(xnT_hi[:, k, tok(b)], xnT_lo[:, k, tok(b)], wh[:, k, :], wl[:, k, :])
                                                     for k in range(DC)])
                    mm.then_inc(rt_z, 1)

            def ffn1():
                slot = ITEMS[NUMBER["w_ffn1", 0]][4] % 2
                weights("w_ffn1", 0)
                pe.wait_ge(ln_lo, 4 * B)
                router(0, wa_hi[:, slot, 0:544].rearrange("p (c n) -> p c n", c=DC),
                       wa_lo[:, slot, 0:544].rearrange("p (c n) -> p c n", c=DC), 136)
                pe.wait_ge(rt_copy, B)
                for b in range(B):
                    pe.wait_ge(mx_mixed, b + 1)
                    pe.transpose(bank[0][:, 0:P], mixed[:, b % 2, 0:P], ident).then_inc(mx_T, 1)
                    pe.wait_ge(mx_lo, b + 1)
                    if b:
                        pe.wait_ge(mx_add, b)
                    passes(bank[1][:, :], [(mixT_hi[:, 0:P], mixT_lo[:, 0:P], wa_hi[:, slot, 544:1056],
                                            wa_lo[:, slot, 544:1056])]).then_inc(mx_y, 1)
                pe.wait_ge(mx_y, B)
                pe.sem_inc(qkv_used, 1)

            def ffn2():
                pe.wait_ge(wgate2_split, 2)
                pe.wait_ge(ln_lo, 6 * B)
                router(1, wgate2_hi[:, :].rearrange("p (c n) -> p c n", c=DC),
                       wgate2_lo[:, :].rearrange("p (c n) -> p c n", c=DC), 8)
                pe.wait_ge(rt_done, 2 * B)
                for e in range(8):
                    slot = ITEMS[NUMBER["w_ffn2", e]][4] % 2
                    weights("w_ffn2", e)
                    wh = wa_hi[:, slot, 0:2048].rearrange("p (c n) -> p c n", c=DC)
                    wl = wa_lo[:, slot, 0:2048].rearrange("p (c n) -> p c n", c=DC)
                    for b in range(B):
                        r = e * B + b
                        if r >= 4:
                            pe.wait_ge(e_tmp, r - 3)
                        passes(bank[r % 4][:, :], [(xnT_hi[:, k, tok(b)], xnT_lo[:, k, tok(b)], wh[:, k, :], wl[:, k, :])
                                                   for k in range(DC)]).then_inc(e_y, 1)
                    pe.wait_ge(e_y, (e + 1) * B)
                    pe.sem_inc(qkv_used, 1)

            def ffn3():
                slot = ITEMS[NUMBER["w_ffn3a", 0]][4] % 2
                weights("w_ffn3a", 0)
                pe.wait_ge(ln_lo, 8 * B)
                router(2, wa_hi[:, slot, 2048:2368].rearrange("p (c n) -> p c n", c=DC),
                       wa_lo[:, slot, 2048:2368].rearrange("p (c n) -> p c n", c=DC), 80)
                weights("w_ffn3b", 1)
                pe.wait_ge(rt_copy, 2 * B)
                bh = wa_hi[:, slot, 0:2048].rearrange("p (c n) -> p c n", c=DC)
                bl = wa_lo[:, slot, 0:2048].rearrange("p (c n) -> p c n", c=DC)
                first = ITEMS[NUMBER["w_ffn3b", 0]][4] % 2
                for b in range(B):
                    pe.wait_ge(mx_mixed, B + b + 1)
                    for k in range(8):
                        mm = pe.transpose(bank[k // 4][:, k % 4 * P:(k % 4 + 1) * P], mixed[:, b % 2, k * P:(k + 1) * P], ident)
                    mm.then_inc(mx_T, 1)
                    if b:
                        pe.wait_ge(mx_add, B + b)
                    passes(bank[2][:, :], [(xnT_hi[:, k, tok(b)], xnT_lo[:, k, tok(b)], bh[:, k, :], bl[:, k, :])
                                           for k in range(DC)], stop=False)
                    pe.wait_ge(mx_lo, B + b + 1)
                    passes(bank[2][:, :], [(mixT_hi[:, k * P:(k + 1) * P], mixT_lo[:, k * P:(k + 1) * P],
                                            wo_hi[:, (first + k // 4) % 2, k % 4 * D:(k % 4 + 1) * D],
                                            wo_lo[:, (first + k // 4) % 2, k % 4 * D:(k % 4 + 1) * D])
                                           for k in range(8)], start=False).then_inc(mx_y, 1)

            pe.wait_ge(const_loaded, 16)
            normed(0)
            narrow(0, "0")
            if phases > 1:
                normed(1)
                ffn0()
            if phases > 2:
                normed(2)
                wide(0, 2, "1", 2)
            if phases > 3:
                normed(3)
                ffn1()
            if phases > 4:
                normed(4)
                narrow(1, "2")
            if phases > 5:
                normed(5)
                ffn2()
            if phases > 6:
                normed(6)
                wide(1, 6, "3", 1)
            if phases > 7:
                normed(7)
                ffn3()

        @block.scalar
        def _(act):
            def norm_root(n):
                act.wait_ge(ln_est, n + 1)
                act.activation(ln_log[:, :], ln_a[:, :], ACT.Ln).then_inc(ln_act, 1)
                act.wait_ge(ln_act, 2 * n + 1)
                act.activation(ln_r0[:, :], ln_log[:, :], ACT.Exp, scale=-0.5).then_inc(ln_act, 1)
                for b in range(B):
                    act.wait_ge(ln_T, n * B + b + 1)
                    act.activation(xnT_hi[:, :, b * S:(b + 1) * S],
                                   bank[4 + b % 4][:, :].rearrange("p (c t) -> p c t", c=DC), ACT.Copy).then_inc(ln_hi, 1)

            def narrow(n, rope):
                def proj_copies(b):
                    act.wait_ge(nb_proj, n * B + b + 1)
                    if b >= 2:
                        act.wait_ge(ng_attn, (n * B + b - 1) * G)
                    act.activation(v_hi[:, b % 2, 0:P], bank[KV][:, P:2 * P], ACT.Copy, scale=UNSCALE).then_inc(nb_vhi, 1)
                    if not rope:
                        if b:
                            act.wait_ge(nb_qkT, n * B + b)
                        act.activation(qn[:, :], bank[Q][:, :], ACT.Copy, scale=UNSCALE).then_inc(nb_qcopy, 1)

                def turned(b):
                    act.wait_ge(nb_qkT, n * B + b + 1)
                    if b >= 2:
                        act.wait_ge(ng_scores, (n * B + b - 1) * G)
                    act.activation(qT_hi[:, b % 2, :], bank[Q][:, :], ACT.Copy, scale=0.25).then_inc(nb_qhi, 1)
                    if b:
                        act.wait_ge(nb_bd, n * B + b)
                    act.activation(kT_hi[:, :], bank[KV][:, :], ACT.Copy).then_inc(nb_khi, 1)

                def soft(j):
                    b, g = divmod(j, G)
                    J = n * UNITS + j
                    act.wait_ge(ng_max, J + 1)
                    if j >= 2:
                        act.wait_ge(ng_probsT, J - 1)
                    if g == 0 and b >= 2:
                        act.wait_ge(nb_inv, n * B + b - 1)
                    for h in range(HPG):
                        op = act.activation(probs[:, j % 2, h * S:(h + 1) * S], bank[S0 + j % 2][:, h * S:(h + 1) * S],
                                            ACT.Exp, bias=negmax[:, j % 2, h:h + 1],
                                            accum_out=total_n[:, b % 2, g * HPG + h:g * HPG + h + 1])
                    op.then_inc(ng_exp, 1)

                def probs_hi(j):
                    J = n * UNITS + j
                    act.wait_ge(ng_probsT, J + 1)
                    if j >= 2:
                        act.wait_ge(ng_attn, J - 1)
                    act.activation(pT_hi[:, j % 2, :], bank[PT0 + j % 2][:, :], ACT.Copy).then_inc(ng_phi, 1)

                def out_hi(b):
                    act.wait_ge(nb_oT, n * B + b + 1)
                    if b:
                        act.wait_ge(nb_out, n * B + b)
                    act.activation(oT_hi[:, :], bank[O + b % 2][:, :], ACT.Copy).then_inc(nb_ohi, 1)

                proj_copies(0)
                turned(0)
                for j in range(UNITS + 8):
                    b, g = divmod(j, G)
                    if 1 <= j <= UNITS:
                        probs_hi(j - 1)
                    if j < UNITS:
                        soft(j)
                    if g == 0 and b + 1 < B:
                        proj_copies(b + 1)
                    if g == 3 and b + 1 < B:
                        turned(b + 1)
                    if g == 4 and b >= 1:
                        out_hi(b - 1)

            def ffn0():
                for v in range(4 * FP):
                    j, ch = v // 4, v // 2 % 2
                    act.wait_ge(f0_gu, v + 1)
                    if v >= 2:
                        act.wait_ge(f0_hid, v - 1)
                    cc = 2 * j + ch
                    act.activation(silu[:, v % 2, :], bank[2 * (v % 2)][:, :], ACT.Silu,
                                   scale=c("gate_s")[:, cc:cc + 1]).then_inc(f0_silu, 1)

            def wide(n, tiles, eps):
                base = n * UNITS
                width = tiles * S

                def step(i, r, seen, last=UNITS):
                    U = i * 16 + (base + r)
                    par, pre = r % 2, (r - 1) % 2
                    if 1 <= seen <= last:
                        act.wait_ge(w_max, U)
                        if seen >= 3:
                            act.wait_ge(w_probsT, U - 2)
                        for h in range(HPG):
                            bk, at = divmod(h * width, 512)
                            src = bank[S0 + bk][:, at:at + width] if tiles == 2 else masked[:, h * S:(h + 1) * S]
                            op = act.activation(probs[:, pre, h * width:(h + 1) * width], src, ACT.Exp,
                                                bias=negmax[:, pre, h:h + 1], accum_out=total[:, pre, h:h + 1])
                        op.then_inc(w_exp, 1)
                    if seen < last:
                        act.wait_ge(w_proj, U + 1)
                        if seen:
                            act.wait_ge(w_newton, U * 4)
                        for h in range(HPG):
                            act.activation(squares[:, h * P:(h + 1) * P], bank[Q][:, h * P:(h + 1) * P], ACT.Square,
                                           accum_out=sumsq[:, h:h + 1])
                        for j in range(tiles):
                            op = act.activation(squares[:, (4 + j) * P:(5 + j) * P], bank[KV][:, 2 * j * P:(2 * j + 1) * P],
                                                ACT.Square, accum_out=sumsq[:, 4 + j:5 + j])
                        op.then_inc(w_sumsq, 1)
                        act.wait_ge(w_newton, U * 4 + 1)
                        act.activation(rms_log[:, 0:4 + tiles], rms_a[:, 0:4 + tiles], ACT.Ln).then_inc(w_log, 1)
                        act.wait_ge(w_log, U + 1)
                        act.activation(rms_r0[:, 0:4 + tiles], rms_log[:, 0:4 + tiles], ACT.Exp, scale=-0.5).then_inc(w_rms0, 1)
                    if 1 <= seen <= last:
                        act.wait_ge(w_probsT, U)
                        if seen >= 2:
                            act.wait_ge(w_attn, U - 1)
                        for j in range(tiles):
                            op = act.activation(pT_hi[:, j, :], bank[PT0 + j][:, :], ACT.Copy)
                        op.then_inc(w_phi, 1)
                    if seen < last:
                        if seen >= 2:
                            act.wait_ge(w_attn, U - 1)
                        act.wait_ge(w_qknorm, U + 1)
                        kv = bank[KV][:, 0:tiles * 256].rearrange("p (j s) -> p j s", j=tiles)
                        act.activation(v_hi[:, par, 0:tiles * P].rearrange("p (j s) -> p j s", j=tiles), kv[:, :, P:2 * P],
                                       ACT.Copy, scale=UNSCALE).then_inc(w_vhi, 1)
                        act.wait_ge(w_qkT, U + 1)
                        if seen:
                            act.wait_ge(w_scores, U)
                        act.activation(qT_hi[:, 0, :], bank[S0][:, :], ACT.Copy, scale=w_comb[:, n:n + 1])
                        act.activation(kT_hi[:, 0:width], bank[S1][:, 0:width], ACT.Copy).then_inc(w_qkhi, 1)
                    if 1 <= seen <= last:
                        act.wait_ge(w_attn, U)
                        if seen >= 2:
                            act.wait_ge(w_out, U - 1)
                        act.activation(oT_hi[:, :], bank[O][:, :], ACT.Copy).then_inc(w_ohi, 1)

                if n == 0:
                    act.wait_ge(w_comb_ready, 4)
                for r in range(16):
                    step(0, r, r)
                with act.Fori(1, UNITS // 16) as i:
                    for r in range(16):
                        step(i, r, 16)
                step(UNITS // 16, 0, UNITS)

            def router(n, E, low, soft):
                for b in range(B):
                    act.wait_ge(rt_z, n * B + b + 1)
                    if low:
                        act.wait_ge(rt_done, n * B + b + 1)
                        act.activation(down[:, b, 0:low], bank[b][:, E:E + low], ACT.Copy, scale=0.5 * UNSCALE).then_inc(rt_copy, 1)
                if soft:
                    act.wait_ge(rt_step, soft)
                    act.activation(expl[:, :, 0:E], rprob[:, :, 0:E], ACT.Exp).then_inc(rt_exp, 1)

            def mix(n, chunks):
                for b in range(B):
                    act.wait_ge(mx_T, n * B + b + 1)
                    if b:
                        act.wait_ge(mx_y, n * B + b)
                    for k in range(0, chunks, 4):
                        w = min(4, chunks - k) * P
                        op = act.activation(mixT_hi[:, k * P:k * P + w], bank[k // 4][:, 0:w], ACT.Copy)
                    op.then_inc(mx_hi, 1)

            def ffn2():
                for r in range(64):
                    e, b = divmod(r, B)
                    act.wait_ge(e_tmp, r + 1)
                    if r >= 2:
                        act.wait_ge(e_add, r - 1)
                    act.activation(hid[:, r % 2, :], ytmp[:, r % 2, :], ACT.Relu, scale=route[:, b, e:e + 1]).then_inc(e_relu, 1)

            act.wait_ge(angles, 11)
            act.activation(trig[:, :, :, :], red[:, :, :, :], ACT.Sin).then_inc(sines, 1)
            act.preload_act_table_set(LOG_EXP)
            for h in range(2):
                act.wait_ge(ctx_loaded[h], 16)
                act.activation(ctxT_hi[:, :, h * 512:(h + 1) * 512], ctx_raw[h].rearrange("p (c t) -> p c t", c=DC),
                               ACT.Copy).then_inc(ctx_hi_split, 1)
            norm_root(0)
            narrow(0, True)
            if phases > 1:
                norm_root(1)
                ffn0()
            if phases > 2:
                act.preload_act_table_set(LOG_EXP)
                norm_root(2)
                wide(0, 2, 1e-6)
            if phases > 3:
                norm_root(3)
                router(0, 8, 128, 2)
                mix(0, 1)
            if phases > 4:
                norm_root(4)
                narrow(1, False)
            if phases > 5:
                norm_root(5)
                ffn2()
            if phases > 6:
                norm_root(6)
                wide(1, 1, 1e-5)
            if phases > 7:
                norm_root(7)
                router(2, 16, 64, 21)
                mix(1, 8)

        @block.vector
        def _(dve):
            def newton(x_, r0, t, r, done, at):
                dve.tensor_tensor(t, r0, r0, ALU.mult).then_inc(done, 1)
                dve.wait_ge(done, at + 1)
                dve.scalar_tensor_tensor(t, t, -0.5, x_, ALU.mult, ALU.mult).then_inc(done, 1)
                dve.wait_ge(done, at + 2)
                dve.scalar_tensor_tensor(r, t, 1.5, r0, ALU.add, ALU.mult).then_inc(done, 1)

            def layer_norm(n):
                for b in range(B):
                    dve.bn_stats(stats[:, b, :], x[:, b, :]).then_inc(ln_aggr, 1)
                dve.wait_ge(ln_aggr, 16 * n + 8)
                for b in range(B):
                    dve.bn_aggr(mv[:, b, :], stats[:, b, :]).then_inc(ln_aggr, 1)
                dve.wait_ge(ln_aggr, 16 * n + 16)
                dve.tensor_scalar(ln_a[:, :], mv[:, :, 1], NORM_EPS, None, ALU.add).then_inc(ln_est, 1)
                dve.wait_ge(ln_est, n + 1)
                dve.wait_ge(ln_act, 2 * n + 2)
                newton(ln_a[:, :], ln_r0[:, :], ln_t[:, :], ln_r[:, :], ln_newton, 3 * n)
                dve.wait_ge(ln_newton, 3 * n + 3)
                for b in range(B + 1):
                    if b < B:
                        if b >= 2:
                            dve.wait_ge(ln_T, n * B + b - 1)
                        dve.tensor_scalar(xn[:, b % 2, :], x[:, b, :], mv[:, b, 0:1], ln_r[:, b:b + 1], ALU.subtract,
                                          ALU.mult).then_inc(ln_norm, 1)
                    if b >= 1:
                        q = b - 1
                        dve.wait_ge(ln_hi, n * B + q + 1)
                        dve.tensor_tensor(xnT_lo[:, :, q * S:(q + 1) * S],
                                          bank[4 + q % 4][:, :].rearrange("p (c t) -> p c t", c=DC),
                                          xnT_hi[:, :, q * S:(q + 1) * S], ALU.subtract).then_inc(ln_lo, 1)

            def rope_tables():
                step = [0]

                def link(op):
                    step[0] += 1
                    op.then_inc(angles, 1)
                    dve.wait_ge(angles, step[0])

                dve.wait_ge(pos_loaded, 16)
                link(dve.tensor_copy(posf[:, :], pos[:, :]))
                for m in range(8):
                    inv = float(np.float32(1.0) / np.float32(ROPE_THETA) ** np.float32(np.float32(2 * m) / np.float32(ND)))
                    dve.tensor_scalar(angle[:, :, 1, m], posf[:, :], inv, None, ALU.mult)
                    op = dve.tensor_scalar(angle[:, :, 0, m], posf[:, :], inv, None, ALU.mult)
                link(op)
                link(dve.tensor_scalar(turns[:, :, 0, :], angle[:, :, 0, :], float(1 / (2 * np.pi)), 0.25, ALU.mult, ALU.add))
                link(dve.tensor_scalar(turns[:, :, 1, :], angle[:, :, 1, :], float(1 / (2 * np.pi)), None, ALU.mult))
                link(dve.tensor_scalar(turns[:, :, :, :], turns[:, :, :, :], ROUND, None, ALU.add))
                link(dve.tensor_scalar(turns[:, :, :, :], turns[:, :, :, :], -ROUND, None, ALU.add))
                for part in (TWO_PI_HI, TWO_PI_MID, TWO_PI_LO):
                    link(dve.scalar_tensor_tensor(angle[:, :, :, :], turns[:, :, :, :], -part, angle[:, :, :, :],
                                                  ALU.mult, ALU.add))
                link(dve.tensor_scalar(angle[:, :, 0, :], angle[:, :, 0, :], float(np.pi / 2), None, ALU.add))
                dve.tensor_scalar(red[:, :, :, :], angle[:, :, :, :], float(np.float32(3.1415925)),
                                  -float(np.float32(3.1415925)), ALU.min, ALU.max).then_inc(angles, 1)
                dve.wait_ge(sines, 1)
                for hf in range(2):
                    dve.tensor_scalar(cosw[:, :, hf * 8:(hf + 1) * 8], trig[:, :, 0, :], UNSCALE, None, ALU.mult)
                dve.tensor_scalar(sinw[:, :, 0:8], trig[:, :, 1, :], -UNSCALE, None, ALU.mult)
                dve.tensor_scalar(sinw[:, :, 8:16], trig[:, :, 1, :], UNSCALE, None, ALU.mult).then_inc(angles, 1)
                dve.wait_ge(angles, 12)

            def narrow(n, rope):
                def heads(ap, h):
                    return ap.rearrange("p (h d) -> p h d", h=h)

                def q_k(b):
                    BB = n * B + b
                    dve.wait_ge(nb_vhi, BB + 1)
                    dve.scalar_tensor_tensor(v_lo[:, b % 2, 0:P], bank[KV][:, P:2 * P], UNSCALE, v_hi[:, b % 2, 0:P],
                                             ALU.mult, ALU.subtract).then_inc(nb_vlo, 1)
                    if rope:
                        cs, sn = cosw[:, b, :].unsqueeze(1), sinw[:, b, :].unsqueeze(1)
                        for src, ra, rb, h in ((bank[Q][:, :], rope_a, rope_b, 32), (bank[KV][:, 0:P], ropek_a[:, :], ropek_b[:, :], 8)):
                            s3, a3, b3 = heads(src, h), heads(ra, h), heads(rb, h)
                            dve.tensor_tensor(a3, s3, cs.broadcast_to([P, h, ND]), ALU.mult)
                            dve.tensor_tensor(b3[:, :, 0:8], s3[:, :, 8:16], sn[:, :, 0:8].broadcast_to([P, h, 8]), ALU.mult)
                            op = dve.tensor_tensor(b3[:, :, 8:16], s3[:, :, 0:8], sn[:, :, 8:16].broadcast_to([P, h, 8]),
                                                   ALU.mult)
                        op.then_inc(nb_rope, 1)
                        dve.wait_ge(nb_rope, b + 1)
                        if b:
                            dve.wait_ge(nb_qkT, BB)
                        dve.tensor_tensor(qn[:, :], rope_a, rope_b, ALU.add)
                        dve.tensor_tensor(kn[:, :].rearrange("p (g h d) -> p g h d", g=G, h=HPG),
                                          heads(ropek_a[:, :], G).unsqueeze(2).broadcast_to([P, G, HPG, ND]),
                                          heads(ropek_b[:, :], G).unsqueeze(2).broadcast_to([P, G, HPG, ND]),
                                          ALU.add).then_inc(nb_qk, 1)
                    else:
                        if b:
                            dve.wait_ge(nb_qkT, BB)
                        dve.tensor_scalar(kn[:, :].rearrange("p (g h d) -> p g h d", g=G, h=HPG),
                                          heads(bank[KV][:, 0:P], G).unsqueeze(2).broadcast_to([P, G, HPG, ND]),
                                          UNSCALE, None, ALU.mult).then_inc(nb_qk, 1)

                def turned(b):
                    BB = n * B + b
                    dve.wait_ge(nb_qhi, BB + 1)
                    dve.scalar_tensor_tensor(qT_lo[:, b % 2, :], bank[Q][:, :], 0.25, qT_hi[:, b % 2, :], ALU.mult,
                                             ALU.subtract).then_inc(nb_qlo, 1)
                    dve.wait_ge(nb_khi, BB + 1)
                    dve.tensor_tensor(kT_lo[:, :], bank[KV][:, :], kT_hi[:, :], ALU.subtract).then_inc(nb_klo, 1)

                def row_max(j):
                    J = n * UNITS + j
                    dve.wait_ge(ng_scores, J + 1)
                    if j >= 2:
                        dve.wait_ge(ng_exp, J - 1)
                    dve.tensor_reduce(negmax[:, j % 2, :], heads(bank[S0 + j % 2][:, :], HPG), AXX, ALU.max,
                                      negate=True).then_inc(ng_max, 1)

                def probs_lo(j):
                    J = n * UNITS + j
                    dve.wait_ge(ng_phi, J + 1)
                    dve.tensor_tensor(pT_lo[:, j % 2, :], bank[PT0 + j % 2][:, :], pT_hi[:, j % 2, :],
                                      ALU.subtract).then_inc(ng_plo, 1)

                def normalise(b):
                    BB = n * B + b
                    dve.wait_ge(ng_attn, (BB + 1) * G)
                    dve.reciprocal(inv_total_n[:, :], total_n[:, b % 2, :]).then_inc(nb_inv, 1)
                    dve.wait_ge(nb_inv, BB + 1)
                    if b:
                        dve.wait_ge(nb_oT, BB)
                    dve.tensor_tensor(heads(on[:, :], 32), heads(bank[O + b % 2][:, :], 32),
                                      inv_total_n[:, :].unsqueeze(2).broadcast_to([P, 32, ND]), ALU.mult).then_inc(nb_on, 1)

                def out_lo(b):
                    BB = n * B + b
                    dve.wait_ge(nb_ohi, BB + 1)
                    dve.tensor_tensor(oT_lo[:, :], bank[O + b % 2][:, :], oT_hi[:, :], ALU.subtract).then_inc(nb_olo, 1)

                def add(b):
                    BB = n * B + b
                    dve.wait_ge(nb_out, BB + 1)
                    dve.scalar_tensor_tensor(x[:, b, :], bank[O + b % 2][:, :], UNSCALE, x[:, b, :], ALU.mult,
                                             ALU.add).then_inc(nb_y, 1)

                q_k(0)
                turned(0)
                for j in range(UNITS + 8):
                    b, g = divmod(j, G)
                    if g == 2 and b >= 1:
                        normalise(b - 1)
                    if j < UNITS:
                        row_max(j)
                    if 1 <= j <= UNITS:
                        probs_lo(j - 1)
                    if g == 1 and b + 1 < B:
                        q_k(b + 1)
                    if g == 4 and b + 1 < B:
                        turned(b + 1)
                    if g == 5 and b >= 1:
                        out_lo(b - 1)
                    if g == 7 and b >= 1:
                        add(b - 1)
                dve.wait_ge(nb_y, (n + 1) * B)

            def ffn0():
                def hidden(v):
                    j, ch, hf = v // 4, v // 2 % 2, v % 2
                    cc = 2 * j + ch
                    dve.wait_ge(f0_silu, v + 1)
                    if v >= 2:
                        dve.wait_ge(f0_split, v - 1)
                    dve.scalar_tensor_tensor(hid[:, v % 2, :], bank[2 * (v % 2) + 1][:, :], c("up_s")[:, cc:cc + 1],
                                             silu[:, v % 2, :], ALU.mult, ALU.mult).then_inc(f0_hid, 1)
                    dve.wait_ge(f0_hid, v + 1)
                    if j >= 2:
                        dve.wait_ge(f0_y, (j - 1) * B)
                    where = slice(hf * 512, (hf + 1) * 512)
                    dve.tensor_copy(hid_hi[:, j % 2, ch, where], hid[:, v % 2, :]).then_inc(f0_split_hi, 1)
                    dve.wait_ge(f0_split_hi, v + 1)
                    dve.tensor_tensor(hid_lo[:, j % 2, ch, where], hid[:, v % 2, :], hid_hi[:, j % 2, ch, where],
                                      ALU.subtract).then_inc(f0_split, 1)

                def add(r):
                    b = r % B
                    dve.wait_ge(f0_y, r + 1)
                    if r >= 2:
                        dve.wait_ge(f0_add, r - 1)
                    dve.tensor_tensor(ytmp[:, r % 2, :], bank[4 + r % 4][:, :], c("down_s"), ALU.mult).then_inc(f0_scaled, 1)
                    dve.wait_ge(f0_scaled, r + 1)
                    if r >= B:
                        dve.wait_ge(f0_add, r - B + 1)
                    dve.tensor_tensor(x[:, b, :], x[:, b, :], ytmp[:, r % 2, :], ALU.add).then_inc(f0_add, 1)

                for v in range(4 * FP + 4):
                    if v < 4 * FP:
                        hidden(v)
                    if v >= 4:
                        add(2 * (v - 4))
                        add(2 * (v - 4) + 1)
                dve.wait_ge(f0_add, FP * B)

            def wide(n, tiles, eps):
                base = n * UNITS
                width = tiles * S
                nq = 4 + tiles

                def step(i, r, seen, last=UNITS):
                    U = i * 16 + (base + r)
                    par, pre = r % 2, (r - 1) % 2
                    if 1 <= seen <= last:
                        dve.wait_ge(w_scores, U)
                        if tiles == 2:
                            if seen >= 3:
                                dve.wait_ge(w_exp, U - 2)
                            for k in range(2):
                                op = dve.tensor_reduce(negmax[:, pre, 2 * k:2 * k + 2],
                                                       bank[S0 + k][:, :].rearrange("p (h t) -> p h t", h=2), AXX, ALU.max,
                                                       negate=True)
                        else:
                            if seen >= 2:
                                dve.wait_ge(w_exp, U - 1)
                            dve.tensor_tensor(masked[:, :].rearrange("p (h t) -> p h t", h=HPG),
                                              bank[S0][:, :].rearrange("p (h t) -> p h t", h=HPG),
                                              c("mask").unsqueeze(1).broadcast_to([P, HPG, S]), ALU.add).then_inc(w_masked, 1)
                            dve.wait_ge(w_masked, U - base)
                            op = dve.tensor_reduce(negmax[:, pre, :], masked[:, :].rearrange("p (h t) -> p h t", h=HPG),
                                                   AXX, ALU.max, negate=True)
                        op.then_inc(w_max, 1)
                        dve.wait_ge(w_exp, U)
                        dve.reciprocal(inv_total[:, pre, :], total[:, pre, :]).then_inc(w_inv, 1)
                        dve.wait_ge(w_inv, U)
                        for h in range(HPG):
                            pr = probs[:, pre, h * width:(h + 1) * width]
                            op = dve.tensor_scalar(pr, pr, inv_total[:, pre, h:h + 1], None, ALU.mult)
                        op.then_inc(w_pnorm, 1)
                    if seen < last:
                        dve.wait_ge(w_sumsq, U + 1)
                        dve.tensor_scalar(rms_a[:, 0:nq], sumsq[:, 0:nq], 1.0 / P, eps * WSCALE * WSCALE, ALU.mult,
                                          ALU.add).then_inc(w_newton, 1)
                        dve.wait_ge(w_rms0, U + 1)
                        newton(rms_a[:, 0:nq], rms_r0[:, 0:nq], rms_t[:, 0:nq], rms_r[:, 0:nq], w_newton, U * 4 + 1)
                        dve.wait_ge(w_newton, U * 4 + 4)
                        if seen:
                            dve.wait_ge(w_qkT, U)
                        dve.tensor_tensor(qn[:, :].rearrange("p (h d) -> p h d", h=HPG),
                                          bank[Q][:, :].rearrange("p (h d) -> p h d", h=HPG),
                                          rms_r[:, 0:4].unsqueeze(2).broadcast_to([P, HPG, P]), ALU.mult)
                        kv = bank[KV][:, 0:tiles * 256].rearrange("p (j s) -> p j s", j=tiles)
                        dve.tensor_tensor(kn[:, 0:tiles * P].rearrange("p (j d) -> p j d", j=tiles), kv[:, :, 0:P],
                                          rms_r[:, 4:nq].unsqueeze(2).broadcast_to([P, tiles, P]),
                                          ALU.mult).then_inc(w_qknorm, 1)
                    if 1 <= seen <= last:
                        dve.wait_ge(w_phi, U)
                        for j in range(tiles):
                            op = dve.tensor_tensor(pT_lo[:, j, :], bank[PT0 + j][:, :], pT_hi[:, j, :], ALU.subtract)
                        op.then_inc(w_plo, 1)
                    if seen < last:
                        dve.wait_ge(w_vhi, U + 1)
                        kv = bank[KV][:, 0:tiles * 256].rearrange("p (j s) -> p j s", j=tiles)
                        dve.scalar_tensor_tensor(v_lo[:, par, 0:tiles * P].rearrange("p (j s) -> p j s", j=tiles),
                                                 kv[:, :, P:2 * P], UNSCALE,
                                                 v_hi[:, par, 0:tiles * P].rearrange("p (j s) -> p j s", j=tiles),
                                                 ALU.mult, ALU.subtract).then_inc(w_vlo, 1)
                    if seen >= 2:
                        b = (r - 2) % B
                        dve.wait_ge(w_out, U - 1)
                        dve.scalar_tensor_tensor(x[:, b, :], bank[Y][:, :], UNSCALE, x[:, b, :], ALU.mult,
                                                 ALU.add).then_inc(w_y, 1)
                    if seen < last:
                        dve.wait_ge(w_qkhi, U + 1)
                        dve.scalar_tensor_tensor(qT_lo[:, 0, :], bank[S0][:, :], w_comb[:, n:n + 1], qT_hi[:, 0, :],
                                                 ALU.mult, ALU.subtract)
                        dve.tensor_tensor(kT_lo[:, 0:width], bank[S1][:, 0:width], kT_hi[:, 0:width],
                                          ALU.subtract).then_inc(w_qklo, 1)
                    if 1 <= seen <= last:
                        dve.wait_ge(w_ohi, U)
                        dve.tensor_tensor(oT_lo[:, :], bank[O][:, :], oT_hi[:, :], ALU.subtract).then_inc(w_olo, 1)

                for r in range(16):
                    step(0, r, r)
                with dve.Fori(1, UNITS // 16) as i:
                    for r in range(16):
                        step(i, r, 16)
                for r in range(2):
                    step(UNITS // 16, r, UNITS + r)
                dve.wait_ge(w_y, base + UNITS)

            rt = [0]

            def route_link(op):
                rt[0] += 1
                op.then_inc(rt_step, 1)
                dve.wait_ge(rt_step, rt[0])

            def router(n, E, bias, low, soft, eps):
                for b in range(B):
                    dve.wait_ge(rt_z, n * B + b + 1)
                    if bias is None:
                        op = dve.tensor_scalar(logits[:, b, 0:E], bank[b][:, 0:E], UNSCALE, None, ALU.mult)
                    else:
                        op = dve.scalar_tensor_tensor(logits[:, b, 0:E], bank[b][:, 0:E], UNSCALE, bias, ALU.mult, ALU.add)
                    op.then_inc(rt_done, 1)
                dve.wait_ge(rt_done, (n + 1) * B)
                lg = logits[:, :, 0:E]
                if soft:
                    route_link(dve.tensor_reduce(rmax[:, :], lg, AXX, ALU.max))
                    route_link(dve.tensor_tensor(rprob[:, :, 0:E], lg, rmax[:, :].unsqueeze(2).broadcast_to([P, B, E]),
                                                 ALU.subtract))
                    dve.wait_ge(rt_exp, soft)
                    route_link(dve.tensor_reduce(rsum[:, :], expl[:, :, 0:E], AXX, ALU.add))
                    route_link(dve.reciprocal(rinv[:, :], rsum[:, :]))
                    route_link(dve.tensor_tensor(rprob[:, :, 0:E], expl[:, :, 0:E],
                                                 rinv[:, :].unsqueeze(2).broadcast_to([P, B, E]), ALU.mult))
                    lg = rprob[:, :, 0:E]
                for b in range(B):
                    op = dve.max(top[:, b, :], lg[:, b, :])
                route_link(op)
                for b in range(B):
                    op = dve.max_index(topi[:, b, :], top[:, b, :], lg[:, b, :])
                route_link(op)
                route_link(dve.tensor_copy(topf[:, :, :], topi[:, :, :]))
                if soft:
                    route_link(dve.tensor_tensor(gsum[:, :], top[:, :, 0], top[:, :, 1], ALU.add))
                    if eps:
                        route_link(dve.tensor_scalar(gsum[:, :], gsum[:, :], eps, None, ALU.add))
                    route_link(dve.reciprocal(ginv[:, :], gsum[:, :]))
                    route_link(dve.tensor_tensor(gates[:, :, :], top[:, :, 0:2],
                                                 ginv[:, :].unsqueeze(2).broadcast_to([P, B, 2]), ALU.mult))
                else:
                    route_link(dve.memset(gates[:, :, :], 0.5))
                for b in range(B):
                    dve.tensor_scalar(pick_a[:, b, 0:E], c("iota")[:, 0:E], topf[:, b, 0:1], gates[:, b, 0:1],
                                      ALU.is_equal, ALU.mult)
                    op = dve.tensor_scalar(pick_b[:, b, 0:E], c("iota")[:, 0:E], topf[:, b, 1:2], gates[:, b, 1:2],
                                           ALU.is_equal, ALU.mult)
                route_link(op)
                route_link(dve.tensor_tensor(route[:, :, 0:E], pick_a[:, :, 0:E], pick_b[:, :, 0:E], ALU.add))

            def mix(n, E, R, scale, bias):
                chunks = E * R // P

                def blend(b):
                    dve.wait_ge(rt_copy, n * B + b + 1)
                    if b >= 2:
                        dve.wait_ge(mx_T, n * B + b - 1)
                    m = mixed[:, b % 2, 0:E * R].rearrange("p (e r) -> p e r", e=E)
                    w = route[:, b, 0:E].unsqueeze(2).broadcast_to([P, E, R])
                    h = (down[:, b, :].rearrange("p (e r) -> p e r", e=E) if E * R == P
                         else down[:, b, 0:R].unsqueeze(1).broadcast_to([P, E, R]))
                    dve.tensor_tensor(m, h, w, ALU.mult).then_inc(mx_mixed, 1)

                blend(0)
                for b in range(B):
                    if b + 1 < B:
                        blend(b + 1)
                    dve.wait_ge(mx_hi, n * B + b + 1)
                    for k in range(0, chunks, 4):
                        w = min(4, chunks - k) * P
                        op = dve.tensor_tensor(mixT_lo[:, k * P:k * P + w], bank[k // 4][:, 0:w], mixT_hi[:, k * P:k * P + w],
                                               ALU.subtract)
                    op.then_inc(mx_lo, 1)
                    dve.wait_ge(mx_y, n * B + b + 1)
                    y = bank[1 if n == 0 else 2][:, :]
                    op = dve.scalar_tensor_tensor(x[:, b, :], y, scale, x[:, b, :], ALU.mult, ALU.add)
                    if bias is not None:
                        op.then_inc(mx_tmp, 1)
                        dve.wait_ge(mx_tmp, b + 1)
                        op = dve.tensor_tensor(x[:, b, :], x[:, b, :], bias, ALU.add)
                    op.then_inc(mx_add, 1)
                dve.wait_ge(mx_add, (n + 1) * B)

            def ffn2():
                dve.wait_ge(expert_b_loaded, 16)

                def bias(r):
                    e, b = divmod(r, B)
                    dve.wait_ge(e_y, r + 1)
                    if r >= 2:
                        dve.wait_ge(e_relu, r - 1)
                    dve.scalar_tensor_tensor(ytmp[:, r % 2, :], bank[r % 4][:, :], UNSCALE, expert_b[:, e, :], ALU.mult,
                                             ALU.add).then_inc(e_tmp, 1)

                for r in range(65):
                    if r < 64:
                        bias(r)
                    if r >= 1:
                        q = r - 1
                        dve.wait_ge(e_relu, q + 1)
                        if q >= B:
                            dve.wait_ge(e_add, q - B + 1)
                        dve.tensor_tensor(x[:, q % B, :], x[:, q % B, :], hid[:, q % 2, :], ALU.add).then_inc(e_add, 1)
                dve.wait_ge(e_add, 64)

            dve.wait_ge(const_loaded, 16)
            for m, (a, b_) in enumerate((("q1", "k1"), ("q3", "k3"))):
                dve.tensor_tensor(w_comb[:, m:m + 1], c(a), c(b_), ALU.mult).then_inc(w_comb_ready, 1)
            dve.wait_ge(w_comb_ready, 2)
            for m in range(2):
                dve.tensor_scalar(w_comb[:, m:m + 1], w_comb[:, m:m + 1], float(np.float32(1 / np.sqrt(P))), None,
                                  ALU.mult).then_inc(w_comb_ready, 1)
            rope_tables()
            for h in range(2):
                dve.wait_ge(ctx_hi_split, h + 1)
                dve.tensor_tensor(ctxT_lo[:, :, h * 512:(h + 1) * 512], ctx_raw[h].rearrange("p (c t) -> p c t", c=DC),
                                  ctxT_hi[:, :, h * 512:(h + 1) * 512], ALU.subtract).then_inc(ctx_split, 1)
            dve.wait_ge(x_loaded, 16)
            layer_norm(0)
            narrow(0, True)
            if phases > 1:
                layer_norm(1)
                ffn0()
            if phases > 2:
                layer_norm(2)
                dve.wait_ge(w_comb_ready, 4)
                wide(0, 2, 1e-6)
            if phases > 3:
                layer_norm(3)
                router(0, 8, c("router1_b"), 128, 1, 0.0)
                mix(0, 8, 16, UNSCALE, None)
            if phases > 4:
                layer_norm(4)
                narrow(1, False)
            if phases > 5:
                layer_norm(5)
                router(1, 8, c("router2_b"), 0, 0, 0.0)
                ffn2()
            if phases > 6:
                layer_norm(6)
                wide(1, 1, 1e-5)
            if phases > 7:
                layer_norm(7)
                router(2, 16, None, 64, 2, 1e-6)
                mix(1, 16, 64, UNSCALE, c("base_b"))


def _chunks(w):
    n = w.shape[1]
    return np.ascontiguousarray(w.reshape(-1, P, n).transpose(1, 0, 2)).reshape(P, -1)


def lay_out(a):
    def qkv(q, k, v):
        return np.concatenate([_chunks(q), _chunks(np.concatenate([k, v], 1))], 1)

    def rows(v):
        return np.broadcast_to(v, (P, v.shape[-1]))

    d = {}
    d["x"] = np.ascontiguousarray(a["x"].transpose(1, 0, 2))
    ct = _chunks(a["ctx_4096"].reshape(T, D).T).reshape(P, DC, 2, 512)
    d["ctxT"] = np.ascontiguousarray(ct.transpose(2, 0, 1, 3)).reshape(2, P, 2048)
    d["pos"] = np.ascontiguousarray(a["itok_BxS2_0_2047"].T)
    for l in ("0", "2"):
        p = f"L{l}_xattn_"
        d["w_qkv" + l] = qkv(a[p + "Wq"], a[p + "Wk"], a[p + "Wv"])[None]
        d["w_out" + l] = _chunks(a[p + "Wo"])[None]
    for l in ("1", "3"):
        p = f"L{l}_xattn_"
        wq, wk, wv, wo = ((a[p + "Wq"], a[p + "Wk"], a[p + "Wv"], a[p + "Wo"]) if l == "1" else
                          (a[p + "q_proj_w"].T, a[p + "k_proj_w"].T, a[p + "v_proj_w"].T, a[p + "o_proj_w"].T))
        d["w_qkv" + l] = np.stack([qkv(wq[:, g * 512:(g + 1) * 512], wk[:, g * P:(g + 1) * P], wv[:, g * P:(g + 1) * P])
                                   for g in range(G)])
        d["w_out" + l] = np.stack([_chunks(wo[g * 512:(g + 1) * 512]) for g in range(G)])
    gt, ut, dt = a["L0_ffn_gate_t"].T, a["L0_ffn_up_t"].T, a["L0_ffn_down_t"].T
    d["w_ffn0"] = np.stack([np.concatenate([_chunks(w[:, (2 * j + ch) * P:(2 * j + ch + 1) * P]) for w in (gt, ut)
                                            for ch in range(2)] + [_chunks(dt[2 * j * P:(2 * j + 2) * P])], 1)
                            for j in range(FP)])
    d["w_ffn1"] = np.concatenate([_chunks(np.concatenate([a["L1_ffn_router_w"].T, a["L1_ffn_A"].reshape(P, D).T], 1)),
                                  a["L1_ffn_Bm"].transpose(0, 2, 1).reshape(P, D)], 1)[None]
    d["w_ffn2"] = np.stack([_chunks(w) for w in a["L2_ffn_W_e"]])
    d["wgate2"] = _chunks(a["L2_ffn_W_gate"])
    d["w_ffn3a"] = np.concatenate([_chunks(a["L3_ffn_base_w"].T),
                                   _chunks(np.concatenate([a["L3_ffn_router_w"].T, a["L3_ffn_A"].T], 1))], 1)[None]
    bt = a["L3_ffn_B"].transpose(0, 2, 1).reshape(1024, D)
    d["w_ffn3b"] = np.stack([_chunks(bt[:512]), _chunks(bt[512:])])
    d["expert_b"] = np.broadcast_to(a["L2_ffn_b_e"], (P, 8, D))
    row = np.arange(P)[:, None]
    cols = {
        "ident": np.eye(P), "head_of_row": (row // ND % HPG == np.arange(HPG)), "iota": np.broadcast_to(np.arange(16), (P, 16)),
        "gate_s": a["L0_ffn_gate_s"].reshape(FC, P).T, "up_s": a["L0_ffn_up_s"].reshape(FC, P).T,
        "down_s": rows(a["L0_ffn_down_s"]), "q1": a["L1_xattn_q_norm_w"][:, None], "k1": a["L1_xattn_k_norm_w"][:, None],
        "q3": a["L3_xattn_q_norm_w"][:, None], "k3": a["L3_xattn_k_norm_w"][:, None], "router1_b": rows(a["L1_ffn_router_b"]),
        "router2_b": rows(a["L2_ffn_b_gate"]), "base_b": rows(a["L3_ffn_base_b"]), "mask": a["mask_1x1xSxS2_ff0"][0, 0],
    }
    d["const"] = np.concatenate([np.asarray(cols[n], np.float32) for n in COLS], 1)
    return {k: np.ascontiguousarray(v) for k, v in d.items()}


def make(nc, arrays, phases=8):
    ins = {}
    for name, v in arrays.items():
        ins[name] = nc.dram_tensor(f"in_{name}_dram", v.shape, mybir.dt.from_np(v.dtype), kind="ExternalInput").ap()
    out = nc.dram_tensor("out_0_dram", (P, B, D), F32, kind="ExternalOutput").ap()
    build(nc, ins, out, phases)


def kernel(**inputs):
    import concourse.bacc as bacc
    from concourse.bass_utils import run_bass_kernel_spmd

    nc = bacc.Bacc("TRN2", target_bir_lowering=False, num_devices=1)
    arrays = lay_out({k: np.asarray(v) for k, v in inputs.items()})
    make(nc, arrays)
    r = run_bass_kernel_spmd(nc, [{f"in_{k}_dram": v for k, v in arrays.items()}], core_ids=[0])
    return np.ascontiguousarray(r.results[0]["out_0_dram"].transpose(1, 0, 2))
```

```python
from contextlib import ExitStack

import numpy as np
import concourse.bass as bass
from concourse import mybir

F32 = mybir.dt.float32
F16 = mybir.dt.float16
I32 = mybir.dt.int32
U32 = mybir.dt.uint32
ALU = mybir.AluOpType
ACT = mybir.ActivationFunctionType
AXX = mybir.AxisListType.X

P = 128
B = 8
S = 128
T = B * S
D = 512
DC = D // P
G = 8
HPG = 4
ND = 16
FF = 1792
FC = FF // P
FP = FC // 2
UNITS = B * G
CHAINS = UNITS + 3
WSCALE = 64.0
UNSCALE = 1.0 / WSCALE
QKV = DC * (HPG * P) + DC * 2 * P
WOUT = HPG * D
NORM_EPS = 1e-5
LOG_EXP = "natural_log_exp_and_others"
ROPE_THETA = 10000.0
TWO_PI_HI = 6.28125
TWO_PI_MID = float((np.array([2 * np.pi - 6.28125], np.float32).view(np.uint32) & np.uint32(0xFFFFF000)).view(np.float32)[0])
TWO_PI_LO = float(2 * np.pi - 6.28125 - TWO_PI_MID)
ROUND = 1.5 * 2.0 ** 23

COLS = {}
_at = 0
for _name, _n in (("ident", P), ("head_of_row", HPG), ("iota", 16), ("gate_s", FC), ("up_s", FC),
                  ("down_s", D), ("q1", 1), ("k1", 1), ("q3", 1), ("k3", 1), ("router1_b", 8),
                  ("router2_b", 8), ("base_b", D), ("mask", S)):
    COLS[_name] = (_at, _at + _n)
    _at += _n
NCONST = _at


def weight_items():
    items, qkv, out = [], 0, 0

    def a(name, i, n, scaled=True):
        nonlocal qkv
        items.append((name, i, n, "qkv", qkv, scaled))
        qkv += 1

    def o(name, i, n, scaled=True):
        nonlocal out
        items.append((name, i, n, "out", out, scaled))
        out += 1

    a("w_qkv0", 0, QKV)
    o("w_out0", 0, WOUT)
    for j in range(FP):
        a("w_ffn0", j, 2048, False)
        o("w_ffn0d", j, 1024, False)
    for g in range(G):
        a("w_qkv1", g, QKV)
        o("w_out1", g, WOUT)
    a("w_ffn1", 0, 544 + 512)
    a("w_qkv2", 0, QKV)
    o("w_out2", 0, WOUT)
    for e in range(8):
        a("w_ffn2", e, 2048)
    for g in range(G):
        a("w_qkv3", g, QKV)
        o("w_out3", g, WOUT)
    a("w_ffn3a", 0, 2048 + 320)
    o("w_ffn3b", 0, 2048)
    a("w_ffn3b", 1, 2048)
    return items


ITEMS = weight_items()
NUMBER = {(name, i): k for k, (name, i, *_rest) in enumerate(ITEMS)}


def build(nc, ins, out):
    ctx = ExitStack()
    with ctx:
        def sb(name, shape, dt):
            return ctx.enter_context(nc.sbuf_tensor(name, [P] + shape, dt))

        def sem(name):
            return ctx.enter_context(nc.semaphore(name))

        x = sb("x", [B, D], F32)
        xn = sb("xn", [2, D], F32)
        xnT_hi, xnT_lo = sb("xnT_hi", [DC, T], F16), sb("xnT_lo", [DC, T], F16)
        ctxT_hi, ctxT_lo = sb("ctxT_hi", [DC, T], F16), sb("ctxT_lo", [DC, T], F16)
        const = sb("const", [NCONST], F32)
        expert_b = sb("expert_b", [8, D], F32)
        wgate2 = sb("wgate2", [DC * 8], F32)
        wgate2_hi, wgate2_lo = sb("wgate2_hi", [DC * 8], F16), sb("wgate2_lo", [DC * 8], F16)
        pos = sb("pos", [B], I32)
        raw = sb("raw", [2, QKV], F32)
        wa_hi, wa_lo = sb("wa_hi", [2, QKV], F16), sb("wa_lo", [2, QKV], F16)
        wo_hi, wo_lo = sb("wo_hi", [2, WOUT], F16), sb("wo_lo", [2, WOUT], F16)
        stats = sb("stats", [B, 6], F32)
        mv = sb("mv", [B, 2], F32)
        ln_log, ln_r0, ln_t, ln_r = (sb(n, [B], F32) for n in ("ln_log", "ln_r0", "ln_t", "ln_r"))
        ln_a = sb("ln_a", [B], F32)
        qn = sb("qn", [D], F32)
        kn = sb("kn", [D], F32)
        probs = sb("probs", [2, HPG * 2 * S], F32)
        pT_hi, pT_lo = sb("pT_hi", [2, HPG * S], F16), sb("pT_lo", [2, HPG * S], F16)
        v_hi, v_lo = sb("v_hi", [4, 2 * P], F16), sb("v_lo", [4, 2 * P], F16)
        qT_hi, qT_lo = sb("qT_hi", [2, HPG * S], F16), sb("qT_lo", [2, HPG * S], F16)
        kT_hi, kT_lo = sb("kT_hi", [4 * S], F16), sb("kT_lo", [4 * S], F16)
        oT_hi, oT_lo = sb("oT_hi", [HPG * S], F16), sb("oT_lo", [HPG * S], F16)
        negmax = sb("negmax", [2, HPG], F32)
        squares = sb("squares", [6 * P], F32)
        sq_hi, sq_lo = qT_hi[:, 0, :], qT_lo[:, 0, :]
        ones16 = sb("ones16", [1], F16)
        sumsq = sb("sumsq", [2], F32)
        rms_log, rms_r0, rms_t, rms_a = (sb(n, [6], F32) for n in ("rms_log", "rms_r0", "rms_t", "rms_a"))
        rms_r = sb("rms_r", [8, 6], F32)
        rawmax = sb("rawmax", [HPG], F32)
        total = sb("total", [2, HPG], F32)
        inv_total = sb("inv_total", [2, HPG], F32)
        w_comb = sb("w_comb", [2], F32)
        masked = sb("masked", [HPG * S], F32)
        bd_hi, bd_lo = sb("bd_hi", [2, 4 * HPG * S], F16), sb("bd_lo", [2, 4 * HPG * S], F16)
        qh_hi, qh_lo = bd_hi, bd_lo
        ctx_raw = [t[:, :, :].rearrange("p a b -> p (a b)").bitcast(F32) for t in (bd_hi, bd_lo)]
        rope_ab = sb("rope_ab", [2, D], F32)
        rope_a, rope_b = rope_ab[:, 0, :], rope_ab[:, 1, :]
        ropek_a, ropek_b = sb("ropek_a", [P], F32), sb("ropek_b", [P], F32)
        posf = sb("posf", [B], F32)
        angle, turns, red = (sb(n, [B, 2, 8], F32) for n in ("angle", "turns", "red"))
        trig = sb("trig", [B, 2, 8], F32)
        cosw, sinw = sb("cosw", [B, ND], F32), sb("sinw", [B, ND], F32)
        total_n = sb("total_n", [2, 32], F32)
        inv_total_n = sb("inv_total_n", [32], F32)
        on = masked
        silu = rope_ab
        hid = sb("hid", [2, D], F32)
        xn_slot = [xn[:, 0, :], xn[:, 1, :], hid[:, 0, :], hid[:, 1, :]]
        hid_hi, hid_lo = (t[:, :, :].rearrange("p s (c t) -> p s c t", c=2) for t in (bd_hi, bd_lo))
        ytmp = xn
        logits = sb("logits", [B, 16], F32)
        expl = sb("expl", [B, 16], F32)
        rprob = sb("rprob", [B, 16], F32)
        rmax, rsum, rinv = sb("rmax", [B], F32), sb("rsum", [B], F32), sb("rinv", [B], F32)
        top = sb("top", [B, 8], F32)
        topi = sb("topi", [B, 8], U32)
        topf = sb("topf", [B, 8], F32)
        gsum, ginv = sb("gsum", [B], F32), sb("ginv", [B], F32)
        gates = sb("gates", [B, 2], F32)
        pick_a, pick_b, route = sb("pick_a", [B, 16], F32), sb("pick_b", [B, 16], F32), sb("route", [B, 16], F32)
        down = hid[:, :, :].rearrange("p s (c r) -> p (s c) r", r=P)
        mixed = probs


        def mixT(n, b):
            pair = [t[:, :, :].rearrange("p a b -> p (a b)") for t in ((pT_hi, pT_lo) if n == 0 or b % 2 else (v_hi, v_lo))]
            return [t[:, b % 2 * P:(b % 2 + 1) * P] if n == 0 else t for t in pair]

        def q_bank(p):
            return bank[S0 if p in (1, 3) else Q]

        def quad(q):
            return bank[q][:, :].rearrange("p (b c) -> p b c", b=4)


        bank = [ctx.enter_context(nc.psum_tensor(f"bank{i}", [P, 512], F32)) for i in range(8)]
        Q, KV, S0, S1, PT0, PT1, O, Y = range(8)

        def c(name):
            a, b = COLS[name]
            return const[:, a:b]

        ident = c("ident")

        x_loaded, const_loaded, expert_b_loaded, pos_loaded, wgate2_loaded = (
            sem(n) for n in ("x_loaded", "const_loaded", "expert_b_loaded", "pos_loaded", "wgate2_loaded"))
        ctx_loaded = [sem(f"ctx_loaded{i}") for i in range(2)]
        raw_loaded = [sem(f"raw_loaded{i}") for i in range(2)]
        hi_split, split_done = sem("hi_split"), sem("split_done")
        ctx_hi_split, ctx_split, wgate2_split = sem("ctx_hi_split"), sem("ctx_split"), sem("wgate2_split")
        qkv_used, out_used = sem("qkv_used"), sem("out_used")
        w_comb_ready = sem("w_comb_ready")
        ln_aggr, ln_est, ln_act, ln_newton, ln_norm, ln_T, ln_hi, ln_lo = (
            sem(n) for n in ("ln_aggr", "ln_est", "ln_act", "ln_newton", "ln_norm", "ln_T", "ln_hi", "ln_lo"))
        (w_kvproj, w_qproj, w_kT, w_sums, w_scores, w_probsT, w_attn, w_out) = (
            sem("w_" + n) for n in ("kvproj", "qproj", "kT", "sums", "scores", "probsT", "attn", "outp"))
        w_sqlo = sem("w_sqlo")
        (w_exp, w_sqq, w_log, w_rms0, w_vhi, w_phi, w_qhi, w_khi, w_ohi) = (
            sem("w_" + n) for n in ("exp", "sqq", "log", "rms0", "vhi", "phi", "qhi", "khi", "ohi"))
        (w_masked, w_rowmax, w_max, w_inv, w_pnorm, w_meank, w_meanq, w_newton, w_vlo, w_plo, w_qlo, w_klo, w_olo, w_y) = (
            sem("w_" + n) for n in ("masked", "rowmax", "max", "inv", "pnorm", "meank", "meanq", "newton", "vlo", "plo",
                                    "qlo", "klo", "olo", "y"))
        (nb_proj, nb_qkT, nb_oT, nb_out) = (sem("nb_" + n) for n in ("proj", "qkT", "oT", "outp"))
        (ng_scores, ng_probsT, ng_attn) = (sem("ng_" + n) for n in ("scores", "probsT", "attn"))
        (nb_vhi, nb_qcopy, nb_qhi, nb_khi, nb_ohi, ng_exp, ng_phi) = (
            sem(n) for n in ("nb_vhi", "nb_qcopy", "nb_qhi", "nb_khi", "nb_ohi", "ng_exp", "ng_phi"))
        (nb_vlo, nb_rope, nb_qk, nb_qlo, nb_klo, nb_bd, nb_inv, nb_on, nb_olo, nb_y, ng_max, ng_plo) = (
            sem(n) for n in ("nb_vlo", "nb_rope", "nb_qk", "nb_qlo", "nb_klo", "nb_bd", "nb_inv", "nb_on", "nb_olo",
                             "nb_y", "ng_max", "ng_plo"))
        angles, sines = sem("angles"), sem("sines")
        f0_gu, f0_y, f0_silu, f0_hid, f0_split, f0_scaled, f0_add = (
            sem("f0_" + n) for n in ("gu", "y", "silu", "hid", "split", "scaled", "add"))
        f0_split_hi = sem("f0_split_hi")
        rt_z, rt_copy, rt_step, rt_exp, rt_done = (sem("rt_" + n) for n in ("z", "copy", "step", "exp", "done"))
        mx_mixed, mx_T, mx_hi, mx_lo, mx_y, mx_add, base_b_added = (
            sem("mx_" + n) for n in ("mixed", "T", "hi", "lo", "y", "add", "base_b_added"))
        e_y, e_tmp, e_relu, e_add = (sem("e_" + n) for n in ("y", "tmp", "relu", "add"))
        stored = sem("stored")

        block = ctx.enter_context(nc.Block())
        @block.sync
        def _(sp):
            sp.dma_start(pos[:, :], ins["pos"]).then_inc(pos_loaded, 16)
            sp.dma_start(x[:, :, :], ins["x"]).then_inc(x_loaded, 16)
            sp.dma_start(raw[:, 0, :], ins["w_qkv0"][0]).then_inc(raw_loaded[0], 16)
            sp.dma_start(const[:, :], ins["const"]).then_inc(const_loaded, 16)

            def load(k, name, i):
                dst = raw[:, k % 2, 0:ITEMS[k][2]]
                if not ITEMS[k][5]:
                    dst = dst.bitcast(I32)
                sp.dma_start(dst, ins[name][i]).then_inc(raw_loaded[k % 2], 16)

            for h in range(2):
                sp.dma_start(ctx_raw[h], ins["ctxT"][h]).then_inc(ctx_loaded[h], 16)
            for k, (name, i, n, _, _, _) in enumerate(ITEMS):
                if k == 0:
                    continue
                if k >= 2:
                    sp.wait_ge(split_done, k - 1)
                load(k, name, i)
                if k == 2:
                    sp.dma_start(expert_b[:, :, :], ins["expert_b"]).then_inc(expert_b_loaded, 16)
                    sp.dma_start(wgate2[:, :], ins["wgate2"]).then_inc(wgate2_loaded, 16)
            sp.wait_ge(mx_add, 2 * B)
            sp.dma_start(out, x[:, :, :]).then_inc(stored, 16)
            sp.wait_ge(stored, 16)

        @block.gpsimd
        def _(pool):
            def item(k):
                name, i, n, kind, slot, scaled = ITEMS[k]
                pool.wait_ge(raw_loaded[k % 2], 16 * (k // 2 + 1))
                if slot >= 2:
                    pool.wait_ge(qkv_used if kind == "qkv" else out_used, slot - 1)
                hi, lo = (wa_hi, wa_lo) if kind == "qkv" else (wo_hi, wo_lo)
                hi, lo = hi[:, slot % 2, 0:n], lo[:, slot % 2, 0:n]
                src = raw[:, k % 2, 0:n]
                landed, scale = (src, WSCALE) if scaled else (src.bitcast(I32), 1.0)
                pool.tensor_scalar(hi, landed, scale, 1.0, ALU.mult, ALU.mult)
                pool.tensor_scalar(src, landed, scale, 1.0, ALU.mult, ALU.mult).then_inc(hi_split, 1)
                pool.wait_ge(hi_split, k + 1)
                pool.tensor_tensor(lo, src, hi, ALU.subtract).then_inc(split_done, 1)

            def keys(n, b):
                BB = n * B + b
                if b >= 2:
                    pool.wait_ge(ng_scores, (BB - 1) * G)
                for split, dst, src in ((nb_khi, bd_hi, kT_hi), (nb_klo, bd_lo, kT_lo)):
                    pool.wait_ge(split, BB + 1)
                    dv = dst[:, b % 2, :].rearrange("p (c h t) -> p c h t", c=4, h=HPG)
                    for h in range(HPG):
                        ins_ = pool.tensor_scalar(dv[:, :, h, :], src[:, :].rearrange("p (c t) -> p c t", c=4),
                                                  c("head_of_row")[:, h:h + 1], 1.0, ALU.mult, ALU.mult)
                ins_.then_inc(nb_bd, 1)

            for b in range(B):
                if b < 4:
                    item(b)
                keys(0, b)
            for k in range(4, NUMBER["w_ffn2", 1]):
                item(k)
            pool.wait_ge(wgate2_loaded, 16)
            pool.tensor_scalar(wgate2_hi[:, :], wgate2[:, :], WSCALE, 1.0, ALU.mult, ALU.mult)
            pool.tensor_scalar(wgate2[:, :], wgate2[:, :], WSCALE, 1.0, ALU.mult, ALU.mult).then_inc(wgate2_split, 1)
            pool.wait_ge(wgate2_split, 1)
            pool.tensor_tensor(wgate2_lo[:, :], wgate2[:, :], wgate2_hi[:, :], ALU.subtract).then_inc(wgate2_split, 1)
            for b in range(B):
                keys(1, b)
            for k in range(NUMBER["w_ffn2", 1], len(ITEMS)):
                item(k)
            for b in range(B):
                pool.wait_ge(ln_norm, 7 * B + b + 1)
                pool.tensor_tensor(x[:, b, :], x[:, b, :], c("base_b"), ALU.add).then_inc(base_b_added, 1)

        @block.tensor
        def _(pe):
            def passes(dst, pairs, start=True, stop=True):
                n = 3 * len(pairs)
                k = 0
                for lh, ll, rh, rl in pairs:
                    for l, r in ((lh, rh), (lh, rl), (ll, rh)):
                        mm = pe.matmul(dst, l, r, start=start and k == 0, stop=stop and k == n - 1)
                        k += 1
                return mm

            def tok(b):
                return slice(b * S, (b + 1) * S)

            def normed(n, early=None):
                for b in range(B):
                    pe.wait_ge(ln_norm, n * B + b + 1)
                    if b >= 4:
                        pe.wait_ge(ln_lo, n * B + b - 3)
                    for k in range(DC):
                        mm = pe.transpose(bank[4 + b % 4][:, k * P:(k + 1) * P], xn_slot[b % 4][:, k * P:(k + 1) * P], ident)
                    mm.then_inc(ln_T, 1)
                    if early:
                        early(b)

            def weights(name, i):
                pe.wait_ge(split_done, NUMBER[name, i] + 1)

            def narrow(n, name):
                slot_a, slot_o = ITEMS[NUMBER["w_qkv" + name, 0]][4] % 2, ITEMS[NUMBER["w_out" + name, 0]][4] % 2
                wqh = wa_hi[:, slot_a, 0:2048].rearrange("p (c n) -> p c n", c=DC)
                wql = wa_lo[:, slot_a, 0:2048].rearrange("p (c n) -> p c n", c=DC)
                wkh = wa_hi[:, slot_a, 2048:QKV].rearrange("p (c n) -> p c n", c=DC)
                wkl = wa_lo[:, slot_a, 2048:QKV].rearrange("p (c n) -> p c n", c=DC)

                def proj_q(b, half):
                    if half == 0:
                        pe.wait_ge(ln_lo, 2 * n * 2 * B + b + 1)
                        if b:
                            pe.wait_ge(nb_qlo, n * B + b)
                    passes(bank[Q][:, :], [(xnT_hi[:, k, tok(b)], xnT_lo[:, k, tok(b)], wqh[:, k, :], wql[:, k, :])
                                           for k in (2 * half, 2 * half + 1)], start=half == 0, stop=half == 1)

                def proj_kv(b):
                    if b:
                        pe.wait_ge(nb_klo, n * B + b)
                    mm = passes(bank[KV][:, 0:256], [(ctxT_hi[:, k, tok(b)], ctxT_lo[:, k, tok(b)], wkh[:, k, :],
                                                      wkl[:, k, :]) for k in range(DC)])
                    mm.then_inc(nb_proj, 1)
                    if b == B - 1:
                        pe.wait_ge(nb_proj, (n + 1) * B)
                        pe.sem_inc(qkv_used, 1)

                def turn(b):
                    pe.wait_ge(nb_qk, n * B + b + 1)
                    if n == 1:
                        pe.wait_ge(nb_qcopy, b + 1)
                    pe.wait_ge(nb_vlo, n * B + b + 1)
                    for k in range(4):
                        pe.transpose(bank[Q][:, k * P:(k + 1) * P], qn[:, k * P:(k + 1) * P], ident)
                    for k in range(4):
                        mm = pe.transpose(bank[KV][:, k * P:(k + 1) * P], kn[:, k * P:(k + 1) * P], ident)
                    mm.then_inc(nb_qkT, 1)

                def scores(j):
                    b, g = divmod(j, G)
                    J = n * UNITS + j
                    if g == 0:
                        pe.wait_ge(nb_bd, n * B + b + 1)
                        pe.wait_ge(nb_qlo, n * B + b + 1)
                    if j >= 2:
                        pe.wait_ge(ng_exp, J - 1)
                    ch, m = divmod(g, 2)
                    rows = slice(64 * m, 64 * m + 64)
                    k0 = ch * HPG * S
                    mm = passes(bank[S0 + j % 2][:, :], [(qT_hi[rows, b % 2, ch * P:(ch + 1) * P],
                                                          qT_lo[rows, b % 2, ch * P:(ch + 1) * P],
                                                          bd_hi[rows, b % 2, k0:k0 + 512],
                                                          bd_lo[rows, b % 2, k0:k0 + 512])])
                    mm.then_inc(ng_scores, 1)

                def probs_T(j):
                    J = n * UNITS + j
                    pe.wait_ge(ng_exp, J + 1)
                    if j >= 2:
                        pe.wait_ge(ng_plo, J - 1)
                    for h in range(HPG):
                        mm = pe.transpose(bank[PT0 + j % 2][:, h * S:(h + 1) * S],
                                          probs[:, j % 2, h * S:(h + 1) * S], ident)
                    mm.then_inc(ng_probsT, 1)

                def attend(j):
                    b, g = divmod(j, G)
                    J = n * UNITS + j
                    pe.wait_ge(ng_plo, J + 1)
                    if g == 0:
                        pe.wait_ge(nb_vlo, n * B + b + 1)
                        if b >= 2:
                            pe.wait_ge(nb_y, n * B + b - 1)
                    for h in range(HPG):
                        o = bank[O + b % 2][:, (g * HPG + h) * ND:(g * HPG + h + 1) * ND]
                        vh, vl = v_hi[:, b % 4, g * ND:(g + 1) * ND], v_lo[:, b % 4, g * ND:(g + 1) * ND]
                        mm = passes(o, [(pT_hi[:, j % 2, h * S:(h + 1) * S], pT_lo[:, j % 2, h * S:(h + 1) * S], vh, vl)])
                    mm.then_inc(ng_attn, 1)

                def out_T(b):
                    pe.wait_ge(nb_on, n * B + b + 1)
                    for k in range(4):
                        mm = pe.transpose(bank[O + b % 2][:, k * P:(k + 1) * P], on[:, k * P:(k + 1) * P], ident)
                    mm.then_inc(nb_oT, 1)

                def out_proj(b, half):
                    if half == 0:
                        pe.wait_ge(nb_olo, n * B + b + 1)
                        if b == 0:
                            weights("w_out" + name, 0)
                    wh = wo_hi[:, slot_o, :].rearrange("p (c n) -> p c n", c=DC)
                    wl = wo_lo[:, slot_o, :].rearrange("p (c n) -> p c n", c=DC)
                    mm = passes(bank[O + b % 2][:, :], [(oT_hi[:, k * P:(k + 1) * P], oT_lo[:, k * P:(k + 1) * P],
                                                         wh[:, k, :], wl[:, k, :]) for k in (2 * half, 2 * half + 1)],
                                start=half == 0, stop=half == 1)
                    if half == 1:
                        mm.then_inc(nb_out, 1)
                    if half == 1 and b == B - 1:
                        pe.wait_ge(nb_out, (n + 1) * B)
                        pe.sem_inc(out_used, 1)

                def early(b):
                    if b == 3:
                        weights("w_qkv" + name, 0)
                    if b in (3, 4):
                        proj_q(0, b - 3)
                    if b == 5 and n == 1:
                        proj_kv(0)

                if n == 0:
                    normed(0)
                    for b in (3, 4):
                        early(b)
                else:
                    normed(4, early)
                if n == 0:
                    pe.wait_ge(ctx_split, 2)
                    proj_kv(0)
                turn(0)
                proj_q(1, 0)
                proj_q(1, 1)
                for j in range(UNITS + 10):
                    b, g = divmod(j, G)
                    if j < UNITS:
                        scores(j)
                    if 2 <= j <= UNITS + 1:
                        probs_T(j - 2)
                    if g == 0 and b + 1 < B:
                        proj_kv(b + 1)
                    if g < 2 and b >= 2:
                        out_proj(b - 2, g)
                    if g == 4 and b + 1 < B:
                        turn(b + 1)
                    if g == 6 and b >= 1:
                        out_T(b - 1)
                    if g >= 6 and b + 2 < B:
                        proj_q(b + 2, g - 6)
                    if 3 <= j <= UNITS + 2:
                        attend(j - 3)

            def ffn0():
                def gate_up(v, parts=(0, 1)):
                    j, ch, hf = v // 4, v // 2 % 2, v % 2
                    slot = ITEMS[NUMBER["w_ffn0", j]][4] % 2
                    if v % 4 == 0 and parts[0] == 0:
                        weights("w_ffn0", j)
                    if v >= 2:
                        pe.wait_ge(f0_hid, v - 1)
                    for part in parts:
                        a = part * 1024 + ch * 512
                        mm = passes(bank[2 * (v % 2) + part][:, :],
                                    [(wa_hi[:, slot, a + k * P:a + (k + 1) * P], wa_lo[:, slot, a + k * P:a + (k + 1) * P],
                                      xnT_hi[:, k, hf * 512:(hf + 1) * 512], xnT_lo[:, k, hf * 512:(hf + 1) * 512])
                                     for k in range(DC)])
                    if parts[-1] == 1:
                        mm.then_inc(f0_gu, 1)

                def down_proj(j, b):
                    slot = ITEMS[NUMBER["w_ffn0d", j]][4] % 2
                    r = j * B + b
                    if b == 0:
                        weights("w_ffn0d", j)
                    if b % 4 == 0:
                        pe.wait_ge(f0_split, 4 * j + 3 + b // 4)
                    if r >= 4:
                        pe.wait_ge(f0_scaled, r - 3)
                    mm = passes(bank[4 + r % 4][:, :],
                                [(hid_hi[:, j % 2, ch, tok(b)], hid_lo[:, j % 2, ch, tok(b)],
                                  wo_hi[:, slot, ch * 512:(ch + 1) * 512],
                                  wo_lo[:, slot, ch * 512:(ch + 1) * 512]) for ch in range(2)])
                    mm.then_inc(f0_y, 1)
                    if b == B - 1:
                        pe.wait_ge(f0_y, r + 1)
                        pe.sem_inc(out_used, 1)

                def early(b):
                    if b >= 6:
                        pe.wait_ge(ln_lo, B + 4)
                        gate_up(0, (b - 6,))

                normed(1, early)
                pe.wait_ge(ln_lo, 2 * B)
                for v in range(4 * FP + 4):
                    if 1 <= v < 4 * FP:
                        gate_up(v)
                    if v >= 4:
                        down_proj(v // 4 - 1, 2 * (v % 4))
                        down_proj(v // 4 - 1, 2 * (v % 4) + 1)
                    if v < 4 * FP and v % 4 == 3:
                        pe.wait_ge(f0_gu, v + 1)
                        pe.sem_inc(qkv_used, 1)

            def wide(n, ln, name, tiles):
                par_a, par_o = ITEMS[NUMBER["w_qkv" + name, 0]][4] % 2, ITEMS[NUMBER["w_out" + name, 0]][4] % 2
                k0 = NUMBER["w_qkv" + name, 0]
                width = tiles * S

                def scores(U, s):
                    pe.wait_ge(w_klo, U + 1)
                    if s >= 1:
                        pe.wait_ge(w_exp, U)
                    half, b = s // 4 % 2, s % 4
                    for h in range(HPG):
                        bk, at = divmod(h * width, 512)
                        q = slice(h * 512 + b * S, h * 512 + (b + 1) * S)
                        mm = passes(bank[S0 + bk][:, at:at + width],
                                    [(qh_hi[:, half, q], qh_lo[:, half, q], kT_hi[:, 0:width], kT_lo[:, 0:width])])
                    mm.then_inc(w_scores, 1)

                def project_kv(U, s):
                    b, sl = (s + 1) % B, (par_a + (s + 1) // B) % 2
                    wkh = wa_hi[:, sl, 2048:QKV].rearrange("p (c n) -> p c n", c=DC)
                    wkl = wa_lo[:, sl, 2048:QKV].rearrange("p (c n) -> p c n", c=DC)
                    if s + 4 < UNITS:
                        pe.wait_ge(w_meanq, U + 5)
                    for j in range(tiles):
                        sh, sl_ = (ctxT_hi, ctxT_lo) if j == 0 else (xnT_hi, xnT_lo)
                        mm = passes(bank[KV][:, j * 256:(j + 1) * 256],
                                    [(sh[:, k, tok(b)], sl_[:, k, tok(b)], wkh[:, k, :], wkl[:, k, :]) for k in range(DC)])
                    mm.then_inc(w_kvproj, 1)

                def attend(U, s):
                    pe.wait_ge(w_plo, U)
                    if s >= 2:
                        pe.wait_ge(w_olo, U - 1)
                    v = (s - 1) % 4
                    mm = passes(bank[O][:, :], [(v_hi[:, v, j * P:(j + 1) * P], v_lo[:, v, j * P:(j + 1) * P],
                                                 pT_hi[:, j, :], pT_lo[:, j, :]) for j in range(tiles)])
                    mm.then_inc(w_attn, 1)

                def project_q(i, U, s, parts=(0, 1)):
                    p = s + 5
                    half, h, sl = p // 4 % 2, p % 4, (par_a + p // B) % 2
                    if p % B == 0 and parts[0] == 0:
                        pe.wait_ge(split_done, i * 4 + (k0 + 2 * (p // B) + 1))
                    if p >= 4:
                        pe.wait_ge(w_qlo, U + 5)
                    elif p >= 2:
                        pe.wait_ge(w_qlo, U + 4)
                    where = slice(half * 512, (half + 1) * 512)
                    w = [slice(k * 512 + h * P, k * 512 + (h + 1) * P) for k in range(DC)]
                    mm = passes(q_bank(p)[:, :], [(wa_hi[:, sl, w[k]], wa_lo[:, sl, w[k]], xnT_hi[:, k, where],
                                                 xnT_lo[:, k, where]) for k in range(DC) if k // 2 in parts],
                                start=parts[0] == 0, stop=parts[-1] == 1)
                    if parts[-1] == 1:
                        mm.then_inc(w_qproj, 1)

                def probs_T(U, s):
                    pe.wait_ge(w_pnorm, U + 1)
                    if s >= 1:
                        pe.wait_ge(w_plo, U)
                    pv = probs[:, s % 2, 0:HPG * width].rearrange("p (h j t) -> p h j t", h=HPG, j=tiles)
                    for j in range(tiles):
                        for h in range(HPG):
                            mm = pe.transpose(bank[PT0 + j][:, h * S:(h + 1) * S], pv[:, h, j, :], ident)
                    mm.then_inc(w_probsT, 1)

                def turn_k(U, s):
                    pe.wait_ge(w_vlo, U + 2)
                    for j in range(tiles):
                        mm = pe.transpose(bank[KV][:, j * P:(j + 1) * P], kn[:, j * P:(j + 1) * P], ident)
                    if s + 5 >= UNITS:
                        mm.then_inc(w_kT, 1)

                def sum_q(U, s):
                    pe.wait_ge(w_sqlo, U + 6)
                    if s < -1 and s > -5:
                        pe.wait_ge(w_meanq, U + 5)
                    for b in range(4):
                        for part, sq in enumerate((sq_hi, sq_lo)):
                            mm = pe.matmul(bank[KV][:, 256 + b:257 + b], sq[:, b * P:(b + 1) * P], ones16[:, :],
                                           start=part == 0, stop=part == 1)
                    mm.then_inc(w_sums, 1)

                def out_proj(U, s, i, half):
                    early = 2 if tiles == 2 else 3
                    r = (s - 1) % 16
                    sl = (par_o + r // B) % 2
                    if half == 0:
                        if r % B == 0:
                            pe.wait_ge(split_done, i * 4 + (k0 + 2 * ((s - 1) // B) + 2))
                        pe.wait_ge(w_olo, U)
                        if s >= 2:
                            pe.wait_ge(w_y, U - 1)
                    wh = wo_hi[:, sl, :].rearrange("p (c n) -> p c n", c=DC)
                    wl = wo_lo[:, sl, :].rearrange("p (c n) -> p c n", c=DC)
                    mm = passes(bank[Y][:, :], [(oT_hi[:, h * S:(h + 1) * S], oT_lo[:, h * S:(h + 1) * S],
                                                 wh[:, h, :], wl[:, h, :]) for h in (range(0, early), range(early, HPG))[half]],
                                start=half == 0, stop=half == 1)
                    if half == 1:
                        mm.then_inc(w_out, 1)

                def step(i, s):
                    U = i * 16 + (n * UNITS + s)
                    if s == -1:
                        sum_q(U - 1, s - 1)
                        pe.wait_ge(ln_lo, ln * B + 8)
                    if 0 <= s < UNITS:
                        scores(U, s)
                    if -1 <= s < UNITS - 1:
                        project_kv(U, s)
                    if 1 <= s <= UNITS:
                        attend(U, s)
                    if -1 <= s < UNITS - 1 and (s + 1) % B == B - 1:
                        pe.wait_ge(w_kvproj, U + 2)
                        pe.sem_inc(qkv_used, 1)
                    if s > -5 and s + 5 < UNITS:
                        project_q(i, U, s)
                    if 0 <= s < UNITS and tiles == 2:
                        probs_T(U, s)
                    if 1 <= s <= UNITS:
                        out_proj(U, s, i, 0)
                    if 0 <= s < UNITS and tiles == 1:
                        probs_T(U, s)
                    if -1 <= s < UNITS - 1:
                        turn_k(U, s)
                    if -5 < s < -1:
                        sum_q(U - 1, s - 1)
                    elif -1 <= s < UNITS - 5:
                        sum_q(U, s)
                    if 1 <= s <= UNITS:
                        out_proj(U, s, i, 1)
                        if (s - 1) % B == B - 1:
                            pe.wait_ge(w_out, U)
                            pe.sem_inc(out_used, 1)

                def early(b):
                    if b >= 6:
                        pe.wait_ge(ln_lo, ln * B + 4)
                        project_q(0, n * UNITS - 5, -5, (b - 6,))

                normed(ln, early)
                for s in range(-5, 16):
                    step(0, s)
                with pe.Fori(0, 2) as i:
                    for s in range(16, 32):
                        step(i, s)
                for s in range(48, UNITS + 1):
                    step(0, s)

            def router(n, ln, wh, wl, cols):
                def logits_of(b):
                    pe.wait_ge(ln_lo, ln * B + b + 1)
                    mm = passes(bank[b][:, 0:cols], [(xnT_hi[:, k, tok(b)], xnT_lo[:, k, tok(b)], wh[:, k, :], wl[:, k, :])
                                                     for k in range(DC)])
                    mm.then_inc(rt_z, 1)

                def early(b):
                    if b >= 4:
                        logits_of(b - 4)

                normed(ln, early)
                pe.wait_ge(ln_lo, (ln + 1) * B)
                for b in range(4, B):
                    logits_of(b)

            def turn_mixed(n, b, chunks):
                pe.wait_ge(mx_mixed, n * B + b + 1)
                if n == 1 and b:
                    pe.wait_ge(mx_lo, B + b)
                for k in range(chunks):
                    at = bank[b % 2 if n == 0 else k // 4]
                    mm = pe.transpose(at[:, k % 4 * P:(k % 4 + 1) * P], mixed[:, b % 2, k * P:(k + 1) * P], ident)
                mm.then_inc(mx_T, 1)

            def ffn1():
                slot = ITEMS[NUMBER["w_ffn1", 0]][4] % 2
                weights("w_ffn1", 0)
                router(0, 3, wa_hi[:, slot, 0:544].rearrange("p (c n) -> p c n", c=DC),
                       wa_lo[:, slot, 0:544].rearrange("p (c n) -> p c n", c=DC), 136)
                pe.wait_ge(rt_copy, B)
                turn_mixed(0, 0, 1)
                for b in range(B):
                    if b + 1 < B:
                        turn_mixed(0, b + 1, 1)
                    pe.wait_ge(mx_lo, b + 1)
                    if b >= 2:
                        pe.wait_ge(mx_add, b - 1)
                    hi, lo = mixT(0, b)
                    passes(bank[2 + b % 2][:, :], [(hi, lo, wa_hi[:, slot, 544:1056],
                                                    wa_lo[:, slot, 544:1056])]).then_inc(mx_y, 1)
                pe.wait_ge(mx_y, B)
                pe.sem_inc(qkv_used, 1)

            def ffn2():
                pe.wait_ge(wgate2_split, 2)
                router(1, 5, wgate2_hi[:, :].rearrange("p (c n) -> p c n", c=DC),
                       wgate2_lo[:, :].rearrange("p (c n) -> p c n", c=DC), 8)
                pe.wait_ge(rt_done, 2 * B)
                for e in range(8):
                    slot = ITEMS[NUMBER["w_ffn2", e]][4] % 2
                    weights("w_ffn2", e)
                    wh = wa_hi[:, slot, 0:2048].rearrange("p (c n) -> p c n", c=DC)
                    wl = wa_lo[:, slot, 0:2048].rearrange("p (c n) -> p c n", c=DC)
                    for b in range(B):
                        r = e * B + b
                        if r >= 4:
                            pe.wait_ge(e_tmp, r - 3)
                        passes(bank[r % 4][:, :], [(xnT_hi[:, k, tok(b)], xnT_lo[:, k, tok(b)], wh[:, k, :], wl[:, k, :])
                                                   for k in range(DC)]).then_inc(e_y, 1)
                    pe.wait_ge(e_y, (e + 1) * B)
                    pe.sem_inc(qkv_used, 1)

            def ffn3():
                slot = ITEMS[NUMBER["w_ffn3a", 0]][4] % 2
                zh = wa_hi[:, slot, 2048:2368].rearrange("p (c n) -> p c n", c=DC)
                zl = wa_lo[:, slot, 2048:2368].rearrange("p (c n) -> p c n", c=DC)

                def logits_of(b):
                    if b == 0:
                        weights("w_ffn3a", 0)
                    pe.wait_ge(ln_lo, 7 * B + b + 1)
                    mm = passes(quad(b // 4)[:, b % 4, 0:80], [(xnT_hi[:, k, tok(b)], xnT_lo[:, k, tok(b)], zh[:, k, :],
                                                                zl[:, k, :]) for k in range(DC)])
                    if b % 4 == 3:
                        mm.then_inc(rt_z, 1)

                def early(b):
                    if b >= 3:
                        logits_of(b - 3)

                normed(7, early)
                for b in range(5, B):
                    logits_of(b)
                bh = wa_hi[:, slot, 0:2048].rearrange("p (c n) -> p c n", c=DC)
                bl = wa_lo[:, slot, 0:2048].rearrange("p (c n) -> p c n", c=DC)
                low = [(wh[:, ITEMS[NUMBER["w_ffn3b", i]][4] % 2, :], wl[:, ITEMS[NUMBER["w_ffn3b", i]][4] % 2, :])
                       for i, (wh, wl) in enumerate(((wo_hi, wo_lo), (wa_hi, wa_lo)))]

                def base(b):
                    passes(bank[2 + b % 6][:, :], [(xnT_hi[:, k, tok(b)], xnT_lo[:, k, tok(b)], bh[:, k, :], bl[:, k, :])
                                                   for k in range(DC)], stop=False)

                for b in range(6):
                    base(b)
                weights("w_ffn3b", 1)
                pe.wait_ge(rt_copy, B + 2)
                turn_mixed(1, 0, 8)
                for b in range(B):
                    if b + 1 < B:
                        turn_mixed(1, b + 1, 8)
                    pe.wait_ge(mx_lo, B + b + 1)
                    hi, lo = mixT(1, b)
                    passes(bank[2 + b % 6][:, :], [(hi[:, k * P:(k + 1) * P], lo[:, k * P:(k + 1) * P],
                                                    low[k // 4][0][:, k % 4 * D:(k % 4 + 1) * D],
                                                    low[k // 4][1][:, k % 4 * D:(k % 4 + 1) * D])
                                                   for k in range(8)], start=False).then_inc(mx_y, 1)
                    if b in (1, 2):
                        pe.wait_ge(mx_add, B + b)
                        base(b + 5)

            pe.wait_ge(const_loaded, 16)
            narrow(0, "0")
            ffn0()
            wide(0, 2, "1", 2)
            ffn1()
            narrow(1, "2")
            ffn2()
            wide(1, 6, "3", 1)
            ffn3()

        @block.scalar
        def _(act):
            def norm_root(n):
                act.wait_ge(ln_est, n + 1)
                act.activation(ln_log[:, :], ln_a[:, :], ACT.Ln).then_inc(ln_act, 1)
                act.wait_ge(ln_act, 2 * n + 1)
                act.activation(ln_r0[:, :], ln_log[:, :], ACT.Exp, scale=-0.5).then_inc(ln_act, 1)
                for b in range(B):
                    act.wait_ge(ln_T, n * B + b + 1)
                    act.activation(xnT_hi[:, :, b * S:(b + 1) * S],
                                   bank[4 + b % 4][:, :].rearrange("p (c t) -> p c t", c=DC), ACT.Copy).then_inc(ln_hi, 1)

            def narrow(n, rope):
                def proj_copies(b):
                    act.wait_ge(nb_proj, n * B + b + 1)
                    if b >= 4:
                        act.wait_ge(ng_attn, (n * B + b - 3) * G)
                    act.activation(v_hi[:, b % 4, 0:P], bank[KV][:, P:2 * P], ACT.Copy, scale=UNSCALE).then_inc(nb_vhi, 1)
                    if not rope:
                        if b:
                            act.wait_ge(nb_qkT, n * B + b)
                        act.activation(qn[:, :], bank[Q][:, :], ACT.Copy, scale=UNSCALE).then_inc(nb_qcopy, 1)

                def turned(b):
                    act.wait_ge(nb_qkT, n * B + b + 1)
                    if b >= 2:
                        act.wait_ge(ng_scores, (n * B + b - 1) * G)
                    act.activation(qT_hi[:, b % 2, :], bank[Q][:, :], ACT.Copy, scale=0.25).then_inc(nb_qhi, 1)
                    if b:
                        act.wait_ge(nb_bd, n * B + b)
                    act.activation(kT_hi[:, :], bank[KV][:, :], ACT.Copy).then_inc(nb_khi, 1)

                def soft(j):
                    b, g = divmod(j, G)
                    J = n * UNITS + j
                    act.wait_ge(ng_max, J + 1)
                    if j >= 2:
                        act.wait_ge(ng_probsT, J - 1)
                    if g == 0 and b >= 2:
                        act.wait_ge(nb_inv, n * B + b - 1)
                    for h in range(HPG):
                        op = act.activation(probs[:, j % 2, h * S:(h + 1) * S], bank[S0 + j % 2][:, h * S:(h + 1) * S],
                                            ACT.Exp, bias=negmax[:, j % 2, h:h + 1],
                                            accum_out=total_n[:, b % 2, g * HPG + h:g * HPG + h + 1])
                    op.then_inc(ng_exp, 1)

                def probs_hi(j):
                    J = n * UNITS + j
                    act.wait_ge(ng_probsT, J + 1)
                    if j >= 2:
                        act.wait_ge(ng_attn, J - 1)
                    act.activation(pT_hi[:, j % 2, :], bank[PT0 + j % 2][:, :], ACT.Copy).then_inc(ng_phi, 1)

                def out_hi(b):
                    act.wait_ge(nb_oT, n * B + b + 1)
                    if b:
                        act.wait_ge(nb_out, n * B + b)
                    act.activation(oT_hi[:, :], bank[O + b % 2][:, :], ACT.Copy).then_inc(nb_ohi, 1)

                proj_copies(0)
                turned(0)
                for j in range(UNITS + 7):
                    b, g = divmod(j, G)
                    if 2 <= j <= UNITS + 1:
                        probs_hi(j - 2)
                    if j < UNITS:
                        soft(j)
                    if g == 0 and b + 1 < B:
                        proj_copies(b + 1)
                    if g == 4 and b + 1 < B:
                        turned(b + 1)
                    if g == 6 and b >= 1:
                        out_hi(b - 1)

            def ffn0():
                for v in range(4 * FP):
                    j, ch = v // 4, v // 2 % 2
                    act.wait_ge(f0_gu, v + 1)
                    if v >= 2:
                        act.wait_ge(f0_hid, v - 1)
                    cc = 2 * j + ch
                    act.activation(silu[:, v % 2, :], bank[2 * (v % 2)][:, :], ACT.Silu,
                                   scale=c("gate_s")[:, cc:cc + 1]).then_inc(f0_silu, 1)

            def wide(n, tiles):
                width = tiles * S
                nr = 4 + tiles

                def step(i, s):
                    U = i * 16 + (n * UNITS + s)
                    chain = i * 16 + (n * CHAINS + s + 5)
                    par, ring = s % 2, (s // 4 * 4 - 4) % 8
                    has_k, has_q = -1 <= s < UNITS - 1, -4 <= s and s + 4 < UNITS
                    def soft():
                        if 0 <= s < UNITS:
                            act.wait_ge(w_max, U + 1)
                            if s >= 2:
                                act.wait_ge(w_probsT, U - 1)
                            for h in range(HPG):
                                bk, at = divmod(h * width, 512)
                                if tiles == 2:
                                    src, scale = bank[S0 + bk][:, at:at + width], rms_r[:, ring + h, s % 4:s % 4 + 1]
                                else:
                                    src, scale = masked[:, h * S:(h + 1) * S], 1.0
                                op = act.activation(probs[:, par, h * width:(h + 1) * width], src, ACT.Exp,
                                                    bias=negmax[:, par, h:h + 1], scale=scale, accum_out=total[:, par, h:h + 1])
                            op.then_inc(w_exp, 1)

                    def keys():
                        if has_k:
                            act.wait_ge(w_kvproj, U + 2)
                            if s >= 0:
                                act.wait_ge(w_meank, U + 1)
                            for j in range(tiles):
                                act.activation(squares[:, (4 + j) * P:(5 + j) * P], bank[KV][:, 2 * j * P:(2 * j + 1) * P],
                                               ACT.Square, accum_out=sumsq[:, j:j + 1])
                            if s >= 3:
                                act.wait_ge(w_attn, U - 2)
                            kv = bank[KV][:, 0:tiles * 256].rearrange("p (j s) -> p j s", j=tiles)
                            act.activation(v_hi[:, (s + 1) % 4, 0:width].rearrange("p (j s) -> p j s", j=tiles), kv[:, :, P:2 * P],
                                           ACT.Copy, scale=UNSCALE).then_inc(w_vhi, 1)

                    def roots():
                        if has_k or has_q:
                            if has_k:
                                act.wait_ge(w_meank, U + 2)
                            else:
                                act.wait_ge(w_meanq, U + 5)
                            lo, hi = 0 if has_q else 4, nr if has_k else 4
                            act.activation(rms_log[:, lo:hi], rms_a[:, lo:hi], ACT.Ln).then_inc(w_log, 1)
                            act.wait_ge(w_log, chain)
                            act.activation(rms_r0[:, lo:hi], rms_log[:, lo:hi], ACT.Exp, scale=-0.5).then_inc(w_rms0, 1)

                    def out_hi():
                        if 1 <= s <= UNITS:
                            act.wait_ge(w_attn, U)
                            if s >= 2:
                                act.wait_ge(w_out, U - 1)
                            act.activation(oT_hi[:, :], bank[O][:, :], ACT.Copy).then_inc(w_ohi, 1)

                    for part in ((soft, keys, roots, out_hi) if tiles == 2 else (keys, out_hi, soft, roots)):
                        part()
                    if s + 5 < UNITS:
                        p = s + 5
                        act.wait_ge(w_qproj, U + 6)
                        if s > -5:
                            act.wait_ge(w_sums, U + 5)
                        act.activation(squares[:, 0:512], q_bank(p)[:, :], ACT.Square, scale=UNSCALE)
                        act.activation(sq_hi, q_bank(p)[:, :], ACT.Square, scale=UNSCALE).then_inc(w_sqq, 1)
                        act.activation(qh_hi[:, p // 4 % 2, p % 4 * 512:(p % 4 + 1) * 512], q_bank(p)[:, :], ACT.Copy,
                                       scale=w_comb[:, n:n + 1]).then_inc(w_qhi, 1)
                    if has_k:
                        if s + 5 < UNITS:
                            act.wait_ge(w_sums, U + 6)
                        else:
                            act.wait_ge(w_kT, n * 4 + s - (UNITS - 5) + 1)
                        act.activation(kT_hi[:, 0:width], bank[KV][:, 0:width], ACT.Copy).then_inc(w_khi, 1)
                    if 0 <= s < UNITS:
                        act.wait_ge(w_probsT, U + 1)
                        for j in range(tiles):
                            op = act.activation(pT_hi[:, j, :], bank[PT0 + j][:, :], ACT.Copy)
                        op.then_inc(w_phi, 1)

                if n == 0:
                    act.wait_ge(w_comb_ready, 4)
                for s in range(-5, 16):
                    step(0, s)
                with act.Fori(0, 2) as i:
                    for s in range(16, 32):
                        step(i, s)
                for s in range(48, UNITS + 1):
                    step(0, s)

            def router(n, E, low, soft):
                if n == 2:
                    for q in range(2):
                        act.wait_ge(rt_done, 2 * B + q + 1)
                        act.activation(down[:, 4 * q:4 * q + 4, 0:low], quad(q)[:, :, E:E + low], ACT.Copy,
                                       scale=0.5 * UNSCALE).then_inc(rt_copy, 1)
                elif low:
                    for b in range(B):
                        act.wait_ge(rt_done, n * B + b + 1)
                        act.activation(down[:, b, 0:low], bank[b][:, E:E + low], ACT.Copy, scale=0.5 * UNSCALE).then_inc(rt_copy, 1)
                if soft:
                    act.wait_ge(rt_step, soft)
                    act.activation(expl[:, :, 0:E], rprob[:, :, 0:E], ACT.Exp).then_inc(rt_exp, 1)

            def mix(n, chunks):
                for b in range(B):
                    act.wait_ge(mx_T, n * B + b + 1)
                    if b >= 2:
                        act.wait_ge(mx_y, n * B + b - 1)
                    for k in range(0, chunks, 4):
                        w = min(4, chunks - k) * P
                        src = bank[b % 2 if n == 0 else k // 4]
                        op = act.activation(mixT(n, b)[0][:, k * P:k * P + w], src[:, 0:w], ACT.Copy)
                    op.then_inc(mx_hi, 1)

            def ffn2():
                for r in range(64):
                    e, b = divmod(r, B)
                    act.wait_ge(e_tmp, r + 1)
                    if r >= 2:
                        act.wait_ge(e_add, r - 1)
                    act.activation(hid[:, r % 2, :], ytmp[:, r % 2, :], ACT.Relu, scale=route[:, b, e:e + 1]).then_inc(e_relu, 1)

            act.wait_ge(angles, 11)
            act.activation(trig[:, :, :, :], red[:, :, :, :], ACT.Sin).then_inc(sines, 1)
            act.preload_act_table_set(LOG_EXP)
            norm_root(0)
            for h in range(2):
                act.wait_ge(ctx_loaded[h], 16)
                act.activation(ctxT_hi[:, :, h * 512:(h + 1) * 512], ctx_raw[h].rearrange("p (c t) -> p c t", c=DC),
                               ACT.Copy).then_inc(ctx_hi_split, 1)
            narrow(0, True)
            norm_root(1)
            ffn0()
            act.preload_act_table_set(LOG_EXP)
            norm_root(2)
            wide(0, 2)
            norm_root(3)
            router(0, 8, 128, 2)
            mix(0, 1)
            norm_root(4)
            narrow(1, False)
            norm_root(5)
            ffn2()
            norm_root(6)
            wide(1, 1)
            norm_root(7)
            router(2, 16, 64, 21)
            mix(1, 8)

        @block.vector
        def _(dve):
            def newton(x_, r0, t, r, done, at):
                dve.tensor_tensor(t, r0, r0, ALU.mult).then_inc(done, 1)
                dve.wait_ge(done, at + 1)
                dve.scalar_tensor_tensor(t, t, -0.5, x_, ALU.mult, ALU.mult).then_inc(done, 1)
                dve.wait_ge(done, at + 2)
                dve.scalar_tensor_tensor(r, t, 1.5, r0, ALU.add, ALU.mult).then_inc(done, 1)

            def tile_stats(b, written, count):
                dve.wait_ge(written, count)
                dve.bn_stats(stats[:, b, :], x[:, b, :]).then_inc(ln_aggr, 1)

            def layer_norm(n):
                dve.wait_ge(ln_aggr, 16 * n + 8)
                for b in range(B):
                    dve.bn_aggr(mv[:, b, :], stats[:, b, :]).then_inc(ln_aggr, 1)
                dve.wait_ge(ln_aggr, 16 * n + 16)
                dve.tensor_scalar(ln_a[:, :], mv[:, :, 1], NORM_EPS, None, ALU.add).then_inc(ln_est, 1)
                dve.wait_ge(ln_est, n + 1)
                dve.wait_ge(ln_act, 2 * n + 2)
                newton(ln_a[:, :], ln_r0[:, :], ln_t[:, :], ln_r[:, :], ln_newton, 3 * n)
                dve.wait_ge(ln_newton, 3 * n + 3)
                for b in range(B + 2):
                    if b < B:
                        if b >= 4:
                            dve.wait_ge(ln_T, n * B + b - 3)
                        dve.tensor_scalar(xn_slot[b % 4], x[:, b, :], mv[:, b, 0:1], ln_r[:, b:b + 1], ALU.subtract,
                                          ALU.mult).then_inc(ln_norm, 1)
                    if b >= 2:
                        q = b - 2
                        dve.wait_ge(ln_hi, n * B + q + 1)
                        dve.tensor_tensor(xnT_lo[:, :, q * S:(q + 1) * S],
                                          bank[4 + q % 4][:, :].rearrange("p (c t) -> p c t", c=DC),
                                          xnT_hi[:, :, q * S:(q + 1) * S], ALU.subtract).then_inc(ln_lo, 1)

            def rope_tables():
                step = [0]

                def link(op):
                    step[0] += 1
                    op.then_inc(angles, 1)
                    dve.wait_ge(angles, step[0])

                dve.wait_ge(pos_loaded, 16)
                link(dve.tensor_copy(posf[:, :], pos[:, :]))
                for m in range(8):
                    inv = float(np.float32(1.0) / np.float32(ROPE_THETA) ** np.float32(np.float32(2 * m) / np.float32(ND)))
                    dve.tensor_scalar(angle[:, :, 1, m], posf[:, :], inv, None, ALU.mult)
                    op = dve.tensor_scalar(angle[:, :, 0, m], posf[:, :], inv, None, ALU.mult)
                link(op)
                link(dve.tensor_scalar(turns[:, :, 0, :], angle[:, :, 0, :], float(1 / (2 * np.pi)), 0.25, ALU.mult, ALU.add))
                link(dve.tensor_scalar(turns[:, :, 1, :], angle[:, :, 1, :], float(1 / (2 * np.pi)), None, ALU.mult))
                link(dve.tensor_scalar(turns[:, :, :, :], turns[:, :, :, :], ROUND, None, ALU.add))
                link(dve.tensor_scalar(turns[:, :, :, :], turns[:, :, :, :], -ROUND, None, ALU.add))
                for part in (TWO_PI_HI, TWO_PI_MID, TWO_PI_LO):
                    link(dve.scalar_tensor_tensor(angle[:, :, :, :], turns[:, :, :, :], -part, angle[:, :, :, :],
                                                  ALU.mult, ALU.add))
                link(dve.tensor_scalar(angle[:, :, 0, :], angle[:, :, 0, :], float(np.pi / 2), None, ALU.add))
                dve.tensor_scalar(red[:, :, :, :], angle[:, :, :, :], float(np.float32(3.1415925)),
                                  -float(np.float32(3.1415925)), ALU.min, ALU.max).then_inc(angles, 1)
                dve.wait_ge(sines, 1)
                for hf in range(2):
                    dve.tensor_scalar(cosw[:, :, hf * 8:(hf + 1) * 8], trig[:, :, 0, :], UNSCALE, None, ALU.mult)
                dve.tensor_scalar(sinw[:, :, 0:8], trig[:, :, 1, :], -UNSCALE, None, ALU.mult)
                dve.tensor_scalar(sinw[:, :, 8:16], trig[:, :, 1, :], UNSCALE, None, ALU.mult).then_inc(angles, 1)
                dve.wait_ge(angles, 12)

            def narrow(n, rope):
                def heads(ap, h):
                    return ap.rearrange("p (h d) -> p h d", h=h)

                def q_k(b):
                    BB = n * B + b
                    dve.wait_ge(nb_vhi, BB + 1)
                    dve.scalar_tensor_tensor(v_lo[:, b % 4, 0:P], bank[KV][:, P:2 * P], UNSCALE, v_hi[:, b % 4, 0:P],
                                             ALU.mult, ALU.subtract).then_inc(nb_vlo, 1)
                    if rope:
                        cs, sn = cosw[:, b, :].unsqueeze(1), sinw[:, b, :].unsqueeze(1)
                        for src, ra, rb, h in ((bank[Q][:, :], rope_a, rope_b, 32), (bank[KV][:, 0:P], ropek_a[:, :], ropek_b[:, :], 8)):
                            s3, a3, b3 = heads(src, h), heads(ra, h), heads(rb, h)
                            dve.tensor_tensor(a3, s3, cs.broadcast_to([P, h, ND]), ALU.mult)
                            dve.tensor_tensor(b3[:, :, 0:8], s3[:, :, 8:16], sn[:, :, 0:8].broadcast_to([P, h, 8]), ALU.mult)
                            op = dve.tensor_tensor(b3[:, :, 8:16], s3[:, :, 0:8], sn[:, :, 8:16].broadcast_to([P, h, 8]),
                                                   ALU.mult)
                        op.then_inc(nb_rope, 1)

                def spread(b):
                    BB = n * B + b
                    if rope:
                        dve.wait_ge(nb_rope, b + 1)
                        if b:
                            dve.wait_ge(nb_qkT, BB)
                        dve.tensor_tensor(qn[:, :], rope_a, rope_b, ALU.add)
                        dve.tensor_tensor(kn[:, :].rearrange("p (g h d) -> p g h d", g=G, h=HPG),
                                          heads(ropek_a[:, :], G).unsqueeze(2).broadcast_to([P, G, HPG, ND]),
                                          heads(ropek_b[:, :], G).unsqueeze(2).broadcast_to([P, G, HPG, ND]),
                                          ALU.add).then_inc(nb_qk, 1)
                    else:
                        if b:
                            dve.wait_ge(nb_qkT, BB)
                        dve.tensor_scalar(kn[:, :].rearrange("p (g h d) -> p g h d", g=G, h=HPG),
                                          heads(bank[KV][:, 0:P], G).unsqueeze(2).broadcast_to([P, G, HPG, ND]),
                                          UNSCALE, None, ALU.mult).then_inc(nb_qk, 1)

                def turned(b):
                    BB = n * B + b
                    dve.wait_ge(nb_qhi, BB + 1)
                    dve.scalar_tensor_tensor(qT_lo[:, b % 2, :], bank[Q][:, :], 0.25, qT_hi[:, b % 2, :], ALU.mult,
                                             ALU.subtract).then_inc(nb_qlo, 1)
                    dve.wait_ge(nb_khi, BB + 1)
                    dve.tensor_tensor(kT_lo[:, :], bank[KV][:, :], kT_hi[:, :], ALU.subtract).then_inc(nb_klo, 1)

                def row_max(j):
                    J = n * UNITS + j
                    dve.wait_ge(ng_scores, J + 1)
                    if j >= 2:
                        dve.wait_ge(ng_exp, J - 1)
                    dve.tensor_reduce(negmax[:, j % 2, :], heads(bank[S0 + j % 2][:, :], HPG), AXX, ALU.max,
                                      negate=True).then_inc(ng_max, 1)

                def probs_lo(j):
                    J = n * UNITS + j
                    dve.wait_ge(ng_phi, J + 1)
                    dve.tensor_tensor(pT_lo[:, j % 2, :], bank[PT0 + j % 2][:, :], pT_hi[:, j % 2, :],
                                      ALU.subtract).then_inc(ng_plo, 1)

                def normalise(b):
                    BB = n * B + b
                    dve.wait_ge(ng_attn, (BB + 1) * G)
                    dve.reciprocal(inv_total_n[:, :], total_n[:, b % 2, :]).then_inc(nb_inv, 1)
                    dve.wait_ge(nb_inv, BB + 1)
                    if b:
                        dve.wait_ge(nb_oT, BB)
                    dve.tensor_tensor(heads(on[:, :], 32), heads(bank[O + b % 2][:, :], 32),
                                      inv_total_n[:, :].unsqueeze(2).broadcast_to([P, 32, ND]), ALU.mult).then_inc(nb_on, 1)

                def out_lo(b):
                    BB = n * B + b
                    dve.wait_ge(nb_ohi, BB + 1)
                    dve.tensor_tensor(oT_lo[:, :], bank[O + b % 2][:, :], oT_hi[:, :], ALU.subtract).then_inc(nb_olo, 1)

                def add(b):
                    BB = n * B + b
                    dve.wait_ge(nb_out, BB + 1)
                    dve.scalar_tensor_tensor(x[:, b, :], bank[O + b % 2][:, :], UNSCALE, x[:, b, :], ALU.mult,
                                             ALU.add).then_inc(nb_y, 1)

                q_k(0)
                spread(0)
                turned(0)
                for j in range(UNITS + 12):
                    b, g = divmod(j, G)
                    if j < UNITS:
                        row_max(j)
                    if 2 <= j <= UNITS + 1:
                        probs_lo(j - 2)
                    if g == 1 and b + 1 < B:
                        q_k(b + 1)
                    if g == 2 and b >= 2:
                        add(b - 2)
                    if g == 2 and b + 1 < B:
                        spread(b + 1)
                    if g == 3 and b >= 2:
                        tile_stats(b - 2, nb_y, n * B + b - 1)
                    if g == 4 and b >= 1:
                        normalise(b - 1)
                    if g == 4 and b + 1 < B:
                        turned(b + 1)
                    if g == 6 and b >= 1:
                        out_lo(b - 1)
                dve.wait_ge(nb_y, (n + 1) * B)

            def ffn0():
                def hidden(v):
                    j, ch, hf = v // 4, v // 2 % 2, v % 2
                    cc = 2 * j + ch
                    dve.wait_ge(f0_silu, v + 1)
                    if v >= 2:
                        dve.wait_ge(f0_split, v - 1)
                    dve.scalar_tensor_tensor(hid[:, v % 2, :], bank[2 * (v % 2) + 1][:, :], c("up_s")[:, cc:cc + 1],
                                             silu[:, v % 2, :], ALU.mult, ALU.mult).then_inc(f0_hid, 1)
                    dve.wait_ge(f0_hid, v + 1)
                    if j >= 2:
                        dve.wait_ge(f0_y, (j - 1) * B)
                    where = slice(hf * 512, (hf + 1) * 512)
                    dve.tensor_copy(hid_hi[:, j % 2, ch, where], hid[:, v % 2, :]).then_inc(f0_split_hi, 1)
                    dve.wait_ge(f0_split_hi, v + 1)
                    dve.tensor_tensor(hid_lo[:, j % 2, ch, where], hid[:, v % 2, :], hid_hi[:, j % 2, ch, where],
                                      ALU.subtract).then_inc(f0_split, 1)

                def add(r):
                    b = r % B
                    dve.wait_ge(f0_y, r + 1)
                    if r >= 2:
                        dve.wait_ge(f0_add, r - 1)
                    dve.tensor_tensor(ytmp[:, r % 2, :], bank[4 + r % 4][:, :], c("down_s"), ALU.mult).then_inc(f0_scaled, 1)
                    dve.wait_ge(f0_scaled, r + 1)
                    if r >= B:
                        dve.wait_ge(f0_add, r - B + 1)
                    dve.tensor_tensor(x[:, b, :], x[:, b, :], ytmp[:, r % 2, :], ALU.add).then_inc(f0_add, 1)

                for v in range(4 * FP + 4):
                    if v < 4 * FP:
                        hidden(v)
                    if v >= 4:
                        r = 2 * (v - 4)
                        add(r)
                        add(r + 1)
                        if r >= (FP - 1) * B:
                            tile_stats(r % B, f0_add, r + 1)
                            tile_stats(r % B + 1, f0_add, r + 2)
                dve.wait_ge(f0_add, FP * B)

            def wide(n, tiles, eps):
                width = tiles * S
                nr = 4 + tiles

                def step(i, s):
                    U = i * 16 + (n * UNITS + s)
                    chain = i * 16 + (n * CHAINS + s + 5)
                    par, ring = s % 2, (s // 4 * 4 - 4) % 8
                    has_k, has_q = -1 <= s < UNITS - 1, -4 <= s and s + 4 < UNITS
                    def maxima():
                        if 0 <= s < UNITS:
                            root = rms_r[:, ring:ring + 4, s % 4]
                            dve.wait_ge(w_scores, U + 1)
                            if s >= 1:
                                dve.wait_ge(w_exp, U)
                            if tiles == 2:
                                for k in range(2):
                                    op = dve.tensor_reduce(rawmax[:, 2 * k:2 * k + 2],
                                                           bank[S0 + k][:, :].rearrange("p (h t) -> p h t", h=2), AXX, ALU.max,
                                                           negate=True)
                                op.then_inc(w_rowmax, 1)
                                dve.wait_ge(w_rowmax, U + 1)
                                op = dve.tensor_tensor(negmax[:, par, :], rawmax[:, :], root, ALU.mult)
                            else:
                                for h in range(HPG):
                                    op = dve.scalar_tensor_tensor(masked[:, h * S:(h + 1) * S], bank[S0][:, h * S:(h + 1) * S],
                                                                  rms_r[:, ring + h, s % 4:s % 4 + 1], c("mask"), ALU.mult, ALU.add)
                                op.then_inc(w_masked, 1)
                                dve.wait_ge(w_masked, U - n * UNITS + 1)
                                op = dve.tensor_reduce(negmax[:, par, :], masked[:, :].rearrange("p (h t) -> p h t", h=HPG),
                                                       AXX, ALU.max, negate=True)
                            op.then_inc(w_max, 1)

                    def add():
                        if 2 <= s <= UNITS + 1:
                            dve.wait_ge(w_out, U - 1)
                            b = (s - 2) % B
                            dve.scalar_tensor_tensor(x[:, b, :], bank[Y][:, :], UNSCALE, x[:, b, :], ALU.mult,
                                                     ALU.add).then_inc(w_y, 1)

                    def normalise():
                        if 0 <= s < UNITS:
                            dve.wait_ge(w_exp, U + 1)
                            dve.reciprocal(inv_total[:, par, :], total[:, par, :]).then_inc(w_inv, 1)
                            dve.wait_ge(w_inv, U + 1)
                            for h in range(HPG):
                                pr = probs[:, par, h * width:(h + 1) * width]
                                op = dve.tensor_scalar(pr, pr, inv_total[:, par, h:h + 1], None, ALU.mult)
                            op.then_inc(w_pnorm, 1)

                    def mean_k():
                        if has_k:
                            dve.wait_ge(w_vhi, U + 2)
                            dve.tensor_scalar(rms_a[:, 4:nr], sumsq[:, 0:tiles], 1.0 / P, eps * WSCALE * WSCALE, ALU.mult,
                                              ALU.add).then_inc(w_meank, 1)

                    def out_lo():
                        if 1 <= s <= UNITS:
                            dve.wait_ge(w_ohi, U)
                            dve.tensor_tensor(oT_lo[:, :], bank[O][:, :], oT_hi[:, :], ALU.subtract).then_inc(w_olo, 1)

                    for part in ((maxima, add, normalise, mean_k, out_lo) if tiles == 2 else
                                 (maxima, mean_k, add, out_lo, normalise)):
                        part()
                    if has_k or has_q:
                        lo, hi = 0 if has_q else 4, nr if has_k else 4
                        dve.wait_ge(w_rms0, chain)
                        newton(rms_a[:, lo:hi], rms_r0[:, lo:hi], rms_t[:, lo:hi], rms_r[:, s % 8, lo:hi], w_newton,
                               (chain - 1) * 3)
                        dve.wait_ge(w_newton, chain * 3)
                    if has_k:
                        kv = bank[KV][:, 0:tiles * 256].rearrange("p (j s) -> p j s", j=tiles)
                        dve.tensor_tensor(kn[:, 0:width].rearrange("p (j d) -> p j d", j=tiles), kv[:, :, 0:P],
                                          rms_r[:, s % 8, 4:nr].unsqueeze(2).broadcast_to([P, tiles, P]), ALU.mult)
                        v = (s + 1) % 4
                        dve.scalar_tensor_tensor(v_lo[:, v, 0:width].rearrange("p (j s) -> p j s", j=tiles),
                                                 kv[:, :, P:2 * P], UNSCALE,
                                                 v_hi[:, v, 0:width].rearrange("p (j s) -> p j s", j=tiles),
                                                 ALU.mult, ALU.subtract).then_inc(w_vlo, 1)
                    if s + 5 < UNITS:
                        p = s + 5
                        dve.wait_ge(w_sqq, U + 6)
                        dve.tensor_tensor(sq_lo, squares[:, 0:512], sq_hi, ALU.subtract).then_inc(w_sqlo, 1)
                        dve.wait_ge(w_qhi, U + 6)
                        piece = slice(p % 4 * 512, (p % 4 + 1) * 512)
                        dve.scalar_tensor_tensor(qh_lo[:, p // 4 % 2, piece], q_bank(p)[:, :], w_comb[:, n:n + 1],
                                                 qh_hi[:, p // 4 % 2, piece], ALU.mult, ALU.subtract).then_inc(w_qlo, 1)
                    if has_k:
                        dve.wait_ge(w_khi, U + 2)
                        dve.tensor_tensor(kT_lo[:, 0:width], bank[KV][:, 0:width], kT_hi[:, 0:width],
                                          ALU.subtract).then_inc(w_klo, 1)
                    if s + 5 < UNITS:
                        dve.wait_ge(w_sums, U + 6)
                        dve.tensor_scalar(rms_a[:, 0:4], bank[KV][:, 256:260], WSCALE * WSCALE / P, eps * WSCALE * WSCALE, ALU.mult,
                                          ALU.add).then_inc(w_meanq, 1)
                    if 0 <= s < UNITS:
                        dve.wait_ge(w_phi, U + 1)
                        for j in range(tiles):
                            op = dve.tensor_tensor(pT_lo[:, j, :], bank[PT0 + j][:, :], pT_hi[:, j, :], ALU.subtract)
                        op.then_inc(w_plo, 1)

                for s in range(-5, 16):
                    step(0, s)
                with dve.Fori(0, 2) as i:
                    for s in range(16, 32):
                        step(i, s)
                for s in range(48, UNITS + 2):
                    step(0, s)
                    if s >= UNITS - B + 2:
                        tile_stats((s - 2) % B, w_y, n * UNITS + s - 1)
                dve.wait_ge(w_y, (n + 1) * UNITS)

            rt = [0]

            def route_link(op):
                rt[0] += 1
                op.then_inc(rt_step, 1)
                dve.wait_ge(rt_step, rt[0])

            def router(n, E, bias, low, soft, eps):
                if n == 2:
                    for q in range(2):
                        dve.wait_ge(rt_z, 2 * B + q + 1)
                        dve.tensor_scalar(logits[:, 4 * q:4 * q + 4, 0:E], quad(q)[:, :, 0:E], UNSCALE, None,
                                          ALU.mult).then_inc(rt_done, 1)
                    dve.wait_ge(rt_done, 2 * B + 2)
                else:
                    for b in range(B):
                        dve.wait_ge(rt_z, n * B + b + 1)
                        dve.scalar_tensor_tensor(logits[:, b, 0:E], bank[b][:, 0:E], UNSCALE, bias, ALU.mult,
                                                 ALU.add).then_inc(rt_done, 1)
                    dve.wait_ge(rt_done, (n + 1) * B)
                lg = logits[:, :, 0:E]
                if soft:
                    route_link(dve.tensor_reduce(rmax[:, :], lg, AXX, ALU.max))
                    route_link(dve.tensor_tensor(rprob[:, :, 0:E], lg, rmax[:, :].unsqueeze(2).broadcast_to([P, B, E]),
                                                 ALU.subtract))
                    dve.wait_ge(rt_exp, soft)
                    route_link(dve.tensor_reduce(rsum[:, :], expl[:, :, 0:E], AXX, ALU.add))
                    route_link(dve.reciprocal(rinv[:, :], rsum[:, :]))
                    route_link(dve.tensor_tensor(rprob[:, :, 0:E], expl[:, :, 0:E],
                                                 rinv[:, :].unsqueeze(2).broadcast_to([P, B, E]), ALU.mult))
                    lg = rprob[:, :, 0:E]
                for b in range(B):
                    op = dve.max(top[:, b, :], lg[:, b, :])
                route_link(op)
                for b in range(B):
                    op = dve.max_index(topi[:, b, :], top[:, b, :], lg[:, b, :])
                route_link(op)
                route_link(dve.tensor_copy(topf[:, :, :], topi[:, :, :]))
                if soft:
                    route_link(dve.tensor_tensor(gsum[:, :], top[:, :, 0], top[:, :, 1], ALU.add))
                    if eps:
                        route_link(dve.tensor_scalar(gsum[:, :], gsum[:, :], eps, None, ALU.add))
                    route_link(dve.reciprocal(ginv[:, :], gsum[:, :]))
                    route_link(dve.tensor_tensor(gates[:, :, :], top[:, :, 0:2],
                                                 ginv[:, :].unsqueeze(2).broadcast_to([P, B, 2]), ALU.mult))
                else:
                    route_link(dve.memset(gates[:, :, :], 0.5))
                for b in range(B):
                    dve.tensor_scalar(pick_a[:, b, 0:E], c("iota")[:, 0:E], topf[:, b, 0:1], gates[:, b, 0:1],
                                      ALU.is_equal, ALU.mult)
                    op = dve.tensor_scalar(pick_b[:, b, 0:E], c("iota")[:, 0:E], topf[:, b, 1:2], gates[:, b, 1:2],
                                           ALU.is_equal, ALU.mult)
                route_link(op)
                route_link(dve.tensor_tensor(route[:, :, 0:E], pick_a[:, :, 0:E], pick_b[:, :, 0:E], ALU.add))

            def mix(n, E, R, scale):
                chunks = E * R // P

                def blend(b):
                    if n == 0:
                        dve.wait_ge(rt_copy, b + 1)
                    else:
                        dve.wait_ge(rt_copy, B + b // 4 + 1)
                    if b >= 2:
                        dve.wait_ge(mx_T, n * B + b - 1)
                    m = mixed[:, b % 2, 0:E * R].rearrange("p (e r) -> p e r", e=E)
                    w = route[:, b, 0:E].unsqueeze(2).broadcast_to([P, E, R])
                    h = (down[:, b, :].rearrange("p (e r) -> p e r", e=E) if E * R == P
                         else down[:, b, 0:R].unsqueeze(1).broadcast_to([P, E, R]))
                    dve.tensor_tensor(m, h, w, ALU.mult).then_inc(mx_mixed, 1)

                def low(b):
                    dve.wait_ge(mx_hi, n * B + b + 1)
                    hi, lo = mixT(n, b)
                    for k in range(0, chunks, 4):
                        w = min(4, chunks - k) * P
                        src = bank[b % 2 if n == 0 else k // 4]
                        op = dve.tensor_tensor(lo[:, k * P:k * P + w], src[:, 0:w], hi[:, k * P:k * P + w], ALU.subtract)
                    op.then_inc(mx_lo, 1)

                def add(b):
                    if n == 1:
                        dve.wait_ge(base_b_added, b + 1)
                    dve.wait_ge(mx_y, n * B + b + 1)
                    y = bank[2 + (b % 2 if n == 0 else b % 6)][:, :]
                    dve.scalar_tensor_tensor(x[:, b, :], y, scale, x[:, b, :], ALU.mult, ALU.add).then_inc(mx_add, 1)

                blend(0)
                blend(1)
                for b in range(B + 1):
                    if b < B:
                        low(b)
                    if b + 2 < B:
                        blend(b + 2)
                    if b >= 1:
                        add(b - 1)
                    if b >= 2 and n == 0:
                        tile_stats(b - 2, mx_add, b - 1)
                if n == 0:
                    tile_stats(B - 1, mx_add, B)
                dve.wait_ge(mx_add, (n + 1) * B)

            def ffn2():
                dve.wait_ge(expert_b_loaded, 16)

                def bias(r):
                    e, b = divmod(r, B)
                    dve.wait_ge(e_y, r + 1)
                    if r >= 2:
                        dve.wait_ge(e_relu, r - 1)
                    dve.scalar_tensor_tensor(ytmp[:, r % 2, :], bank[r % 4][:, :], UNSCALE, expert_b[:, e, :], ALU.mult,
                                             ALU.add).then_inc(e_tmp, 1)

                for r in range(65):
                    if r < 64:
                        bias(r)
                    if r >= 1:
                        q = r - 1
                        dve.wait_ge(e_relu, q + 1)
                        if q >= B:
                            dve.wait_ge(e_add, q - B + 1)
                        dve.tensor_tensor(x[:, q % B, :], x[:, q % B, :], hid[:, q % 2, :], ALU.add).then_inc(e_add, 1)
                        if q >= 7 * B:
                            tile_stats(q % B, e_add, q + 1)
                dve.wait_ge(e_add, 64)

            rope_tables()
            for b in range(B):
                tile_stats(b, x_loaded, 16)
            layer_norm(0)
            for h in range(2):
                dve.wait_ge(ctx_hi_split, h + 1)
                dve.tensor_tensor(ctxT_lo[:, :, h * 512:(h + 1) * 512], ctx_raw[h].rearrange("p (c t) -> p c t", c=DC),
                                  ctxT_hi[:, :, h * 512:(h + 1) * 512], ALU.subtract).then_inc(ctx_split, 1)
            dve.wait_ge(const_loaded, 16)
            for m, (a, b_) in enumerate((("q1", "k1"), ("q3", "k3"))):
                dve.tensor_tensor(w_comb[:, m:m + 1], c(a), c(b_), ALU.mult).then_inc(w_comb_ready, 1)
            dve.wait_ge(w_comb_ready, 2)
            dve.memset(ones16[:, :], 1.0)
            for m in range(2):
                dve.tensor_scalar(w_comb[:, m:m + 1], w_comb[:, m:m + 1], float(np.float32(1 / np.sqrt(P))), None,
                                  ALU.mult).then_inc(w_comb_ready, 1)
            narrow(0, True)
            layer_norm(1)
            ffn0()
            layer_norm(2)
            dve.wait_ge(w_comb_ready, 4)
            wide(0, 2, 1e-6)
            layer_norm(3)
            router(0, 8, c("router1_b"), 128, 1, 0.0)
            mix(0, 8, 16, UNSCALE)
            layer_norm(4)
            narrow(1, False)
            layer_norm(5)
            router(1, 8, c("router2_b"), 0, 0, 0.0)
            ffn2()
            layer_norm(6)
            wide(1, 1, 1e-5)
            layer_norm(7)
            router(2, 16, None, 64, 2, 1e-6)
            mix(1, 16, 64, UNSCALE)


def _chunks(w):
    n = w.shape[1]
    return np.ascontiguousarray(w.reshape(-1, P, n).transpose(1, 0, 2)).reshape(P, -1)


def lay_out(a):
    def qkv(q, k, v):
        return np.concatenate([_chunks(q), _chunks(np.concatenate([k, v], 1))], 1)

    def rows(v):
        return np.broadcast_to(v, (P, v.shape[-1]))

    d = {}
    d["x"] = np.ascontiguousarray(a["x"].transpose(1, 0, 2))
    ct = _chunks(a["ctx_4096"].reshape(T, D).T).reshape(P, DC, 2, 512)
    d["ctxT"] = np.ascontiguousarray(ct.transpose(2, 0, 1, 3)).reshape(2, P, 2048)
    d["pos"] = np.ascontiguousarray(a["itok_BxS2_0_2047"].T)
    for l in ("0", "2"):
        p = f"L{l}_xattn_"
        d["w_qkv" + l] = qkv(a[p + "Wq"], a[p + "Wk"], a[p + "Wv"])[None]
        d["w_out" + l] = _chunks(a[p + "Wo"])[None]
    for l in ("1", "3"):
        p = f"L{l}_xattn_"
        wq, wk, wv, wo = ((a[p + "Wq"], a[p + "Wk"], a[p + "Wv"], a[p + "Wo"]) if l == "1" else
                          (a[p + "q_proj_w"].T, a[p + "k_proj_w"].T, a[p + "v_proj_w"].T, a[p + "o_proj_w"].T))
        d["w_qkv" + l] = np.stack([qkv(wq[:, g * 512:(g + 1) * 512], wk[:, g * P:(g + 1) * P], wv[:, g * P:(g + 1) * P])
                                   for g in range(G)])
        d["w_out" + l] = np.stack([_chunks(wo[g * 512:(g + 1) * 512]) for g in range(G)])
    gt, ut, dt = a["L0_ffn_gate_t"].T, a["L0_ffn_up_t"].T, a["L0_ffn_down_t"].T
    d["w_ffn0"] = np.stack([np.concatenate([_chunks(w[:, (2 * j + ch) * P:(2 * j + ch + 1) * P]) for w in (gt, ut)
                                            for ch in range(2)], 1) for j in range(FP)])
    d["w_ffn0d"] = np.stack([_chunks(dt[2 * j * P:(2 * j + 2) * P]) for j in range(FP)])
    d["w_ffn1"] = np.concatenate([_chunks(np.concatenate([a["L1_ffn_router_w"].T, a["L1_ffn_A"].reshape(P, D).T], 1)),
                                  a["L1_ffn_Bm"].transpose(0, 2, 1).reshape(P, D)], 1)[None]
    d["w_ffn2"] = np.stack([_chunks(w) for w in a["L2_ffn_W_e"]])
    d["wgate2"] = _chunks(a["L2_ffn_W_gate"])
    d["w_ffn3a"] = np.concatenate([_chunks(a["L3_ffn_base_w"].T),
                                   _chunks(np.concatenate([a["L3_ffn_router_w"].T, a["L3_ffn_A"].T], 1))], 1)[None]
    bt = a["L3_ffn_B"].transpose(0, 2, 1).reshape(1024, D)
    d["w_ffn3b"] = np.stack([_chunks(bt[:512]), _chunks(bt[512:])])
    d["expert_b"] = np.broadcast_to(a["L2_ffn_b_e"], (P, 8, D))
    row = np.arange(P)[:, None]
    cols = {
        "ident": np.eye(P), "head_of_row": (row // ND % HPG == np.arange(HPG)), "iota": np.broadcast_to(np.arange(16), (P, 16)),
        "gate_s": a["L0_ffn_gate_s"].reshape(FC, P).T, "up_s": a["L0_ffn_up_s"].reshape(FC, P).T,
        "down_s": rows(a["L0_ffn_down_s"]), "q1": a["L1_xattn_q_norm_w"][:, None], "k1": a["L1_xattn_k_norm_w"][:, None],
        "q3": a["L3_xattn_q_norm_w"][:, None], "k3": a["L3_xattn_k_norm_w"][:, None], "router1_b": rows(a["L1_ffn_router_b"]),
        "router2_b": rows(a["L2_ffn_b_gate"]), "base_b": rows(a["L3_ffn_base_b"]), "mask": a["mask_1x1xSxS2_ff0"][0, 0],
    }
    d["const"] = np.concatenate([np.asarray(cols[n], np.float32) for n in COLS], 1)
    return {k: np.ascontiguousarray(v) for k, v in d.items()}


def make(nc, arrays):
    ins = {}
    for name, v in arrays.items():
        ins[name] = nc.dram_tensor(f"in_{name}_dram", v.shape, mybir.dt.from_np(v.dtype), kind="ExternalInput").ap()
    out = nc.dram_tensor("out_0_dram", (P, B, D), F32, kind="ExternalOutput").ap()
    build(nc, ins, out)


def kernel(**inputs):
    import concourse.bacc as bacc
    from concourse.bass_utils import run_bass_kernel_spmd

    nc = bacc.Bacc("TRN2", target_bir_lowering=False, num_devices=1)
    arrays = lay_out({k: np.asarray(v) for k, v in inputs.items()})
    make(nc, arrays)
    r = run_bass_kernel_spmd(nc, [{f"in_{k}_dram": v for k, v in arrays.items()}], core_ids=[0])
    return np.ascontiguousarray(r.results[0]["out_0_dram"].transpose(1, 0, 2))
```
